# Optimizing a Trainium2 kernel written in Bass

```python
import numpy as np
import jax
import jax.numpy as jnp

def _softmax(x, axis=-1):
    return jax.nn.softmax(x, axis=axis)

def _gelu(x):
    return jax.nn.gelu(x, approximate=True)

def _silu(x):
    return jax.nn.silu(x)

def _sigmoid(x):
    return jax.nn.sigmoid(x)

def _layernorm(x, axis=-1, eps=1e-05):
    m = jnp.mean(x, axis=axis, keepdims=True)
    v = jnp.var(x, axis=axis, keepdims=True)
    return (x - m) / jnp.sqrt(v + eps)

def _scatter_add(tgt, idx, src, axis=0):
    return tgt.at[idx].add(src)

def _segment_sum(src, seg, n):
    return jax.ops.segment_sum(src, seg, n)
kernel_name = 'mk_vit_tower_cls_d1_tok_img256_r4_722f26'

def setup_inputs(seed: int=0):
    np.random.seed(seed)
    _w = jnp.asarray

    def _rec_inputs():
        import jax
        import jax.numpy as jnp
        _rk = jax.random.key(seed)
        x = -7.10856e-05 + 0.999911 * jax.random.normal(jax.random.fold_in(_rk, 1), (4, 64, 128, 64), jnp.float32)
        cls_tok = 0.02 * jax.random.normal(jax.random.fold_in(_rk, 5), (1, 1, 64), jnp.float32)
        return (x, cls_tok)
    x, cls_tok = _rec_inputs()

    def _L0_tok_setup():
        import jax, jax.numpy as jnp
        import numpy as np
        PATCH_LEN = 16
        STRIDE = 8
        PAD = 8
        key = jax.random.key(seed)
        k1, k2 = jax.random.split(key)
        x = jax.random.normal(k1, (32, 64, 128, 64), dtype=jnp.float32)
        in_feat = 64 * (PATCH_LEN // 2 + 1) * 2
        W = jax.random.normal(k2, (64, in_feat), dtype=jnp.float32) * 0.02
        return {'x': x, 'W': W}
    _L0_tok_all = _L0_tok_setup()
    _L0_tok_in = {k: v for k, v in _L0_tok_all.items() if k in ('W',)}
    del _L0_tok_all

    def _L0_attn_setup():
        import jax, jax.numpy as jnp
        import numpy as np
        import math
        EMBED_DIM = 64
        SEQ_LEN = 1024
        BATCH = 4
        NUM_SCALES = (24.0, 720.0)
        key = jax.random.key(seed)
        ks = jax.random.split(key, 8)
        d = EMBED_DIM
        x = jax.random.normal(ks[0], (BATCH, SEQ_LEN, d), dtype=jnp.float32)
        s = 1.0 / math.sqrt(d)
        Wq = jax.random.uniform(ks[1], (d, d), jnp.float32, -s, s)
        bq = jax.random.uniform(ks[2], (d,), jnp.float32, -s, s)
        Wk = jax.random.uniform(ks[3], (d, d), jnp.float32, -s, s)
        bk = jax.random.uniform(ks[4], (d,), jnp.float32, -s, s)
        Wv = jax.random.uniform(ks[5], (d, d), jnp.float32, -s, s)
        bv = jax.random.uniform(ks[6], (d,), jnp.float32, -s, s)
        beta = jnp.ones((len(NUM_SCALES),), dtype=jnp.float32)
        return {'x': x, 'Wq': Wq, 'bq': bq, 'Wk': Wk, 'bk': bk, 'Wv': Wv, 'bv': bv, 'beta': beta}
    _L0_attn_all = _L0_attn_setup()
    _L0_attn_in = {k: v for k, v in _L0_attn_all.items() if k in ('Wq', 'bq', 'Wk', 'bk', 'Wv', 'bv', 'beta')}
    del _L0_attn_all

    def _L0_ffn_setup():
        import jax, jax.numpy as jnp
        import numpy as np
        TOP_K = 2
        key = jax.random.key(seed)
        ks = jax.random.split(key, 4)
        B, L, D, H, E = (8, 1024, 64, 256, 8)
        s = 0.02
        return {'x': jax.random.normal(ks[0], (B, L, D), jnp.float32), 'Wg': jax.random.normal(ks[1], (D, E), jnp.float32) * s, 'bg': jnp.zeros((E,), jnp.float32), 'W1': jax.random.normal(ks[2], (E, D, H), jnp.float32) * s, 'b1': jnp.zeros((E, H), jnp.float32), 'W2': jax.random.normal(ks[3], (E, H, D), jnp.float32) * s, 'b2': jnp.zeros((E, D), jnp.float32)}
    _L0_ffn_all = _L0_ffn_setup()
    _L0_ffn_in = {k: v for k, v in _L0_ffn_all.items() if k in ('Wg', 'bg', 'W1', 'b1', 'W2', 'b2')}
    del _L0_ffn_all
    return {'x': x, 'cls_tok': cls_tok, 'L0_tok_W': _L0_tok_in['W'], 'L0_attn_Wq': _L0_attn_in['Wq'], 'L0_attn_bq': _L0_attn_in['bq'], 'L0_attn_Wk': _L0_attn_in['Wk'], 'L0_attn_bk': _L0_attn_in['bk'], 'L0_attn_Wv': _L0_attn_in['Wv'], 'L0_attn_bv': _L0_attn_in['bv'], 'L0_attn_beta': _L0_attn_in['beta'], 'L0_ffn_Wg': _L0_ffn_in['Wg'], 'L0_ffn_bg': _L0_ffn_in['bg'], 'L0_ffn_W1': _L0_ffn_in['W1'], 'L0_ffn_b1': _L0_ffn_in['b1'], 'L0_ffn_W2': _L0_ffn_in['W2'], 'L0_ffn_b2': _L0_ffn_in['b2']}

def reference(x, cls_tok, L0_tok_W, L0_attn_Wq, L0_attn_bq, L0_attn_Wk, L0_attn_bk, L0_attn_Wv, L0_attn_bv, L0_attn_beta, L0_ffn_Wg, L0_ffn_bg, L0_ffn_W1, L0_ffn_b1, L0_ffn_W2, L0_ffn_b2):
    import jax
    import jax.numpy as jnp

    def _L0_tok_ref(x, W):
        import jax, jax.numpy as jnp
        import numpy as np
        PATCH_LEN = 16
        STRIDE = 8
        PAD = 8
        B, C, T, V = x.shape
        xp = jnp.pad(x, ((0, 0), (0, 0), (0, PAD), (0, 0)), mode='edge')
        Tp = T + PAD
        N = (Tp - PATCH_LEN) // STRIDE + 1
        idx = jnp.arange(N)[:, None] * STRIDE + jnp.arange(PATCH_LEN)[None, :]
        patches = xp[:, :, idx, :]
        patches = jnp.transpose(patches, (0, 4, 2, 3, 1))
        xf = jnp.fft.rfft(patches, axis=-2, norm='ortho')
        F = xf.shape[-2]
        x_real = xf.real.reshape(B, V, N, F * C)
        x_imag = xf.imag.reshape(B, V, N, F * C)
        x_emb = jnp.concatenate([x_real, x_imag], axis=-1)
        x_emb = x_emb @ W.T
        return x_emb.reshape(B, V * N, -1)

    def _L0_attn_ref(x, Wq, bq, Wk, bk, Wv, bv, beta):
        import jax, jax.numpy as jnp
        import numpy as np
        import math
        EMBED_DIM = 64
        SEQ_LEN = 1024
        BATCH = 4
        NUM_SCALES = (24.0, 720.0)
        d = x.shape[-1]
        seq_len = x.shape[1]
        sqrt_d = jnp.asarray(math.sqrt(d), x.dtype)
        Q = jnp.einsum('bsd,ed->bse', x, Wq) + bq
        K = jnp.einsum('bsd,ed->bse', x, Wk) + bk
        V = jnp.einsum('bsd,ed->bse', x, Wv) + bv
        attn = jnp.einsum('bse,bte->bst', Q, K) / sqrt_d
        idx = jnp.arange(seq_len, dtype=jnp.float32)
        absdiff = jnp.abs(idx[:, None] - idx[None, :])
        two_pi = jnp.asarray(2.0 * math.pi, jnp.float32)
        bias = jnp.zeros((seq_len, seq_len), dtype=jnp.float32)
        for n, T in enumerate(NUM_SCALES):
            bias = bias + beta[n] * jnp.cos(two_pi * absdiff / T)
        scores = jax.nn.softmax(attn + bias[None, :, :], axis=-1)
        return jnp.einsum('bst,bte->bse', scores, V)

    def _L0_ffn_ref(x, Wg, bg, W1, b1, W2, b2):
        import jax, jax.numpy as jnp
        import numpy as np
        TOP_K = 2
        B, L, D = x.shape
        E = W1.shape[0]
        xf = x.reshape(-1, D)
        gate_logits = xf @ Wg + bg
        top_w, top_i = jax.lax.top_k(gate_logits, TOP_K)
        top_w = jax.nn.softmax(top_w, axis=-1)
        w_dense = jnp.sum(jax.nn.one_hot(top_i, E, dtype=xf.dtype) * top_w[..., None], axis=1)
        out = jnp.zeros_like(xf)
        for e in range(E):
            h = jax.nn.gelu(xf @ W1[e] + b1[e], approximate=False)
            out = out + w_dense[:, e:e + 1] * (h @ W2[e] + b2[e])
        return out.reshape(B, L, D)
    h = _L0_tok_ref(x, L0_tok_W)
    h = jnp.concatenate([jnp.broadcast_to(cls_tok, (h.shape[0], 1, h.shape[2])), h], axis=1)
    h = h + _L0_attn_ref(_layernorm(h, axis=-1), L0_attn_Wq, L0_attn_bq, L0_attn_Wk, L0_attn_bk, L0_attn_Wv, L0_attn_bv, L0_attn_beta)
    h = h + _L0_ffn_ref(_layernorm(h, axis=-1), L0_ffn_Wg, L0_ffn_bg, L0_ffn_W1, L0_ffn_b1, L0_ffn_W2, L0_ffn_b2)
    return h

_drawn_inputs = setup_inputs


def setup_inputs(seed=0):
    import zlib

    import numpy as np

    out = dict(_drawn_inputs(seed))
    spreads = {'L0_attn_beta': (1.0, 0.6),
     'L0_ffn_bg': (0.0, 0.1),
     'L0_ffn_b1': (0.0, 0.329),
     'L0_ffn_b2': (0.0, 0.1)}
    factors = {'cls_tok': 34.447, 'L0_attn_bq': 4.957, 'L0_attn_bk': 64.0}
    for name, (base, spread) in spreads.items():
        noise = np.random.default_rng([zlib.crc32(name.encode()), seed]).standard_normal(out[name].shape)
        drawn = base * np.exp(spread * noise) if base else spread * noise
        out[name] = jnp.asarray(drawn.astype(out[name].dtype))
    for name, factor in factors.items():
        out[name] = (out[name] * factor).astype(out[name].dtype)
    return out
```

```python
from contextlib import ExitStack

import numpy as np

import concourse.bass as bass
from concourse import mybir

F32 = mybir.dt.float32
F16 = mybir.dt.float16
ALU = mybir.AluOpType
ACT = mybir.ActivationFunctionType
AX_X = mybir.AxisListType.X

B, C, T, V = 4, 64, 128, 64
PATCH, STRIDE = 16, 8
NP = T // STRIDE
NBLK = NP + 1
NF = 2 * (PATCH // 2 + 1)
D = 64
SEQ = V * NP
TILES = SEQ // 128
CLS = B * SEQ
COLS = CLS + B
E, H = 8, 256
HT = E * H // 128
EPS = 1e-5
WSCALE = 64.0
QSCALE = D ** -0.5
GATE_STEPS = 10
PERIODS = (24.0, 720.0)
XB = NBLK * 4 * V


def build(nc, x, cls_tok, wf, wq, wk, wv, beta, wg, bg, w1, b1, w2, b2,
          dft, ident, qtab, ktab, negmask, before, out):
    ctx = ExitStack()
    with ctx:
        def sb(name, shape, dt=F32):
            return ctx.enter_context(nc.sbuf_tensor(name, shape, dt))

        def sem(name):
            return ctx.enter_context(nc.semaphore(name))

        xs = sb("xs", [128, B * XB])
        P = xs[:, 0:4 * SEQ].rearrange("p (r n) -> p r n", r=4)
        hid = xs[:, 4 * SEQ:8 * SEQ].rearrange("p (r n) -> p r n", r=4)
        wout = xs[:, 8 * SEQ:9 * SEQ].rearrange("p (r t d) -> p r t d", r=2, d=D)
        diff, equal = (xs[:, (9 * SEQ + k * TILES * E * E):(9 * SEQ + (k + 1) * TILES * E * E)]
                       .rearrange("p (t e f) -> p t e f", e=E, f=E) for k in range(2))
        ident32 = sb("ident32", [128, 128])
        ident16 = sb("ident16", [128, 128], F16)
        wf_sb = sb("wf_sb", [NF, 64 * 64])
        dft_sb = sb("dft_sb", [NF, 16])
        G = sb("G", [128, 4, 2, 64])
        parts = sb("parts", [128, SEQ])
        fold = sb("fold", [128, D])
        wq_sb = sb("wq_sb", [D + 1, 128])
        wk_sb = sb("wk_sb", [D + 1, 128])
        wv_sb = sb("wv_sb", [D + 1, D])
        h_tok = sb("h_tok", [128, B * TILES + 1, D])
        centred = sb("centred", [128, TILES, D])
        squares = sb("squares", [128, TILES, D])
        normed = sb("normed", [128, TILES, 2, D])
        stats = sb("stats", [128, 5, TILES])
        half = sb("half", [128, TILES])
        xT = sb("xT", [D + 1, SEQ])
        QA = sb("QA", [128, COLS], F16)
        QB = sb("QB", [128, COLS], F16)
        KA = sb("KA", [128, COLS], F16)
        KB = sb("KB", [128, COLS], F16)
        qtab_sb = sb("qtab_sb", [128, SEQ + B])
        qhi = sb("qhi", [128, SEQ + B], F16)
        qcol = sb("qcol", [128, 2])
        Vt = sb("Vt", [128, B * TILES + 1, D + 1])
        Pc = sb("Pc", [1, SEQ])
        Pz = sb("Pz", [128, B * 33])
        Pzc = sb("Pzc", [1, B])
        mpart = sb("mpart", [128, TILES, 3])
        mneg = sb("mneg", [128, TILES], F16)
        mcls = sb("mcls", [1, 4])
        rden = sb("rden", [128, TILES])
        attn = sb("attn", [128, TILES, D])
        FA = sb("FA", [128, CLS + 512 * 2], F16)
        w1f = sb("w1f", [128, E * H])
        WA = sb("WA", [128, E * H], F16)
        WB = sb("WB", [128, E * H], F16)
        w2_sb = sb("w2_sb", [128, HT, D])
        b1_sb = sb("b1_sb", [128, HT])
        b2_sb = sb("b2_sb", [E, D])
        wgf = sb("wgf", [128, E])
        GA = sb("GA", [128, E], F16)
        GB = sb("GB", [128, E], F16)
        bg_sb = sb("bg_sb", [128, E])
        before_sb = sb("before_sb", [128, E * E])
        logits = sb("logits", [128, TILES, E])
        rank = sb("rank", [128, TILES, E])
        top = sb("top", [128, TILES])
        expd = sb("expd", [128, TILES, E])
        chosen = sb("chosen", [128, TILES, E])
        csum = sb("csum", [128, 2, TILES])
        wcur = sb("wcur", [128, TILES, E])
        wtok = sb("wtok", [128, B * TILES + 1, E])
        wT = sb("wT", [E, SEQ])
        hcls = sb("hcls", [128, HT, B])
        ocls = sb("ocls", [B, E, D])
        scls = sb("scls", [B, D])

        ps = ctx.enter_context(nc.psum_tensor("ps", [128, 8, 512], F32))

        def banks(first, count=1):
            return ps[:, first:first + count, :].rearrange("p b n -> p (b n)")

        x_landed = [sem(f"x_landed{b}") for b in range(B)]
        x_ready = sem("x_ready")
        emb_w_landed = sem("emb_w_landed")
        ident_landed = sem("ident_landed")
        proj_w_landed = sem("proj_w_landed")
        aug_landed = sem("aug_landed")
        ktab_landed = sem("ktab_landed")
        cls_landed = sem("cls_landed")
        ffn_w_landed = sem("ffn_w_landed")
        gate_w_landed = sem("gate_w_landed")
        stored = sem("stored")
        ones_set = sem("ones_set")
        consts_set = sem("consts_set")
        ident16_set = sem("ident16_set")
        emb_w_summed = sem("emb_w_summed")
        emb_w_ready = sem("emb_w_ready")
        qaug_scaled = sem("qaug_scaled")
        qaug_split = sem("qaug_split")
        qaug_ready = sem("qaug_ready")
        w1_hi = sem("w1_hi")
        w1_lo = sem("w1_lo")
        emb_done = sem("emb_done")
        parts_copied = sem("parts_copied")
        tok_done = sem("tok_done")
        tok_copied = sem("tok_copied")
        ln_sum = sem("ln_sum")
        ln_mean = sem("ln_mean")
        ln_centred = sem("ln_centred")
        ln_squared = sem("ln_squared")
        ln_sumsq = sem("ln_sumsq")
        ln_var = sem("ln_var")
        ln_rstd = sem("ln_rstd")
        ln_done = sem("ln_done")
        norm_T = sem("norm_T")
        xT_copied = sem("xT_copied")
        q_done = sem("q_done")
        q_hi = sem("q_hi")
        q_hi_again = sem("q_hi_again")
        q_lo = sem("q_lo")
        k_done = sem("k_done")
        k_hi = sem("k_hi")
        k_hi_again = sem("k_hi_again")
        k_lo = sem("k_lo")
        v_done = sem("v_done")
        v_copied = sem("v_copied")
        side_full = [sem("side_full0"), sem("side_full1")]
        side_free = [sem("side_free0"), sem("side_free1")]
        m_ready = sem("m_ready")
        mcls_max = sem("mcls_max")
        mcls_ready = sem("mcls_ready")
        score_done = sem("score_done")
        exp_done = sem("exp_done")
        clskey_exp = sem("clskey_exp")
        pv_done = sem("pv_done")
        acc_done = sem("acc_done")
        acc_recip = sem("acc_recip")
        acc_free = sem("acc_free")
        attn_added = sem("attn_added")
        cq_scored = sem("cq_scored")
        cq_exp = sem("cq_exp")
        cq_acc = sem("cq_acc")
        f_hi = sem("f_hi")
        f_lo = sem("f_lo")
        gate_done = sem("gate_done")
        gate_step = sem("gate_step")
        gate_exp = sem("gate_exp")
        w_ready = sem("w_ready")
        wtok_copied = sem("wtok_copied")
        wT_done = sem("wT_done")
        wT_copied = sem("wT_copied")
        b2_done = sem("b2_done")
        b2_added = sem("b2_added")
        hid_done = sem("hid_done")
        gelu_done = sem("gelu_done")
        hid_used = sem("hid_used")
        out_weighed = sem("out_weighed")
        out_added = sem("out_added")
        hcls_done = sem("hcls_done")
        hcls_biased = sem("hcls_biased")
        hcls_gelu = sem("hcls_gelu")
        ocls_done = sem("ocls_done")
        ocls_step = sem("ocls_step")

        P_RING, SCORE_RING, HID_RING, OUT_RING = 4, 2, 4, 2

        USES = (12, 11)

        def side(b, n, bank):
            return b * USES[bank] + n + 1 - bank

        def apart(engine):
            engine.wait_ge(consts_set, 2)

        block = ctx.enter_context(nc.Block())

        @block.sync
        def _(sp):
            sp.dma_start(wf_sb[:, :], wf).then_inc(emb_w_landed, 16)
            sp.dma_start(dft_sb[:, :], dft).then_inc(emb_w_landed, 16)
            sp.dma_start(ident32[:, :], ident).then_inc(ident_landed, 16)
            for b in range(B):
                for h in range(2):
                    to = xs[64 * h:64 * h + 64, b * XB:(b + 1) * XB].rearrange("p (j n) -> p j n", n=4 * V)
                    src = x[b].rearrange("c (j h q) v -> h c j (q v)", h=2, q=4)[h]
                    sp.dma_start(to[:, 0:NP, :], src).then_inc(x_landed[b], 16)
                    pad = to[:, NP, :].rearrange("p (q v) -> p q v", q=4)
                    sp.dma_start(pad, x[b, :, T - 1:T, :].broadcast_to([C, 4, V])).then_inc(x_landed[b], 16)
            for b in range(B):
                sp.wait_ge(x_landed[b], 64)
                sp.sem_inc(x_ready, 1)
            with sp.Fori(0, B) as b:
                sp.wait_ge(out_added, b * E + E + OUT_RING)
                sp.dma_start(out[bass.ds(b, 1), 1:SEQ + 1, :].rearrange("a (i p) d -> p (a i) d", p=128),
                             h_tok[:, bass.ds(b * TILES, TILES), :]).then_inc(stored, 16)
            sp.wait_ge(stored, 16 * (B + 1))

        @block.scalar
        def _(act):
            act.dma_start(wq_sb[:, :], wq).then_inc(proj_w_landed, 16)
            act.dma_start(wk_sb[:, :], wk).then_inc(proj_w_landed, 16)
            act.dma_start(wv_sb[:, :], wv).then_inc(proj_w_landed, 16)
            act.dma_start(qtab_sb[96:128, :], qtab).then_inc(aug_landed, 16)
            act.dma_start(qcol[96:128, 0:1], beta).then_inc(aug_landed, 16)
            act.dma_start(qcol[96:128, 1:2], negmask).then_inc(aug_landed, 16)
            act.dma_start(h_tok[0:B, B * TILES, :], cls_tok[0].broadcast_to([B, D])).then_inc(cls_landed, 16)
            for b in range(B):
                act.dma_start(KA[64:128, b * SEQ:(b + 1) * SEQ], ktab[:, 0:SEQ]).then_inc(ktab_landed, 16)
            act.dma_start(KA[64:128, CLS:COLS], ktab[:, SEQ:SEQ + B]).then_inc(ktab_landed, 16)
            w1_d = w1.rearrange("e d h -> d e h")
            for g in range(2):
                act.dma_start(w1f[64 * g:64 * g + 64, :].rearrange("p (e h) -> p e h", e=E), w1_d).then_inc(ffn_w_landed, 16)
            act.dma_start(w2_sb[:, :, :], w2.rearrange("e (j p) d -> p (e j) d", p=128)).then_inc(ffn_w_landed, 16)
            act.dma_start(b1_sb[:, :], b1).then_inc(ffn_w_landed, 16)
            act.dma_start(b2_sb[:, :], b2).then_inc(ffn_w_landed, 16)
            for g in range(2):
                act.dma_start(wgf[64 * g:64 * g + 64, :], wg).then_inc(gate_w_landed, 16)
            act.dma_start(bg_sb[:, :], bg.rearrange("(a e) -> a e", a=1).broadcast_to([128, E])).then_inc(gate_w_landed, 16)
            act.dma_start(before_sb[:, :], before.broadcast_to([128, E * E])).then_inc(gate_w_landed, 16)

            def square(k, rows, tiles):
                act.wait_ge(ln_centred, k + 1)
                nc.scalar.activation(squares[0:rows, 0:tiles, :], centred[0:rows, 0:tiles, :], ACT.Square).then_inc(ln_squared, 1)

            def copy_parts(b, first):
                act.wait_ge(emb_done, b + 1)
                if not first:
                    act.wait_ge(tok_done, b)
                for a in range(2):
                    rows = slice(64 * a, 64 * a + 64)
                    by_patch = banks(0, 3)[rows, V * a:V * (a + NP)].rearrange("p (n v) -> p v n", v=V)
                    nc.scalar.activation(parts[rows, :].rearrange("p (v n) -> p v n", n=NP), by_patch, ACT.Copy).then_inc(parts_copied, 1)

            def project_hi(k, cols, n):
                act.wait_ge(q_done, k + 1)
                nc.scalar.activation(QB[:, cols], banks(6, 2)[:, 0:n], ACT.Copy, scale=QSCALE).then_inc(q_hi, 1)
                act.wait_ge(k_done, k + 1)
                nc.scalar.activation(KB[:, cols], banks(4, 2)[:, 0:n], ACT.Copy).then_inc(k_hi, 1)

            copy_parts(0, True)
            with act.Fori(0, B - 1) as b:
                square(b, 128, TILES)
                copy_parts(b + 1, False)
                project_hi(b, bass.ds(b * SEQ, SEQ), SEQ)
            square(B - 1, 128, TILES)
            project_hi(B - 1, slice((B - 1) * SEQ, B * SEQ), SEQ)
            square(B, B, 1)
            project_hi(B, slice(CLS, COLS), B)
            act.wait_ge(ffn_w_landed, 80)
            nc.scalar.activation(WA[:, :], w1f[:, :], ACT.Copy, scale=WSCALE).then_inc(w1_hi, 1)
            act.wait_ge(gate_w_landed, 64)
            nc.scalar.activation(GA[:, :], wgf[:, :], ACT.Copy, scale=WSCALE).then_inc(w1_hi, 1)


            def row_of_maxima(b):
                for k in range(2):
                    act.wait_ge(side_full[k], side(b, 10, k))
                    nc.scalar.activation(QA[64:65, bass.ds(b * SEQ + 512 * k, 512)], ps[64:65, 6 + k, :],
                                         ACT.Copy).then_inc(side_free[k], 1)

            def exponentials(b):
                act.wait_ge(acc_done, b + 1)
                for k in range(2):
                    act.wait_ge(side_full[k], side(b, 11, k))
                    nc.scalar.activation(Pc[:, 512 * k:512 * k + 512], ps[0:1, 6 + k, :], ACT.Exp).then_inc(side_free[k], 1)
                for t in range(TILES):
                    act.wait_ge(score_done, b * TILES + t + 1)
                    act.wait_ge(pv_done, b * TILES + t + 1)
                    nc.scalar.activation(P[:, t % P_RING, :], banks(2 * (t % 2), 2), ACT.Exp).then_inc(exp_done, 1)

            act.sem_inc(exp_done, SCORE_RING)
            row_of_maxima(0)
            with act.Fori(0, B - 1) as b:
                exponentials(b)
                row_of_maxima(b + 1)
            exponentials(B - 1)
            act.wait_ge(consts_set, 2)
            act.wait_ge(cq_scored, 1)
            diagonal = Pz[:, :].rearrange("p (b r) -> p b r", b=B)[:, :, 0:4 * TILES:4]
            nc.scalar.activation(diagonal, ps[:, 6, 0:B * TILES].rearrange("p (b t) -> p b t", b=B), ACT.Exp).then_inc(cq_exp, 1)
            nc.scalar.activation(Pzc[:, :], ps[0:1, 6, B * TILES:B * TILES + B], ACT.Exp).then_inc(cq_exp, 1)

            def gate(k, cols, rows, tiles):
                square(B + 1 + k, rows, tiles)
                act.wait_ge(norm_T, B + 1 + k + 1)
                nc.scalar.activation(FA[:, cols], banks(0, 2)[:, 0:tiles * rows], ACT.Copy).then_inc(f_hi, 1)
                act.wait_ge(gate_step, GATE_STEPS * k + 3)
                nc.scalar.activation(expd[0:rows, 0:tiles, :], chosen[0:rows, 0:tiles, :], ACT.Exp).then_inc(gate_exp, 1)

            with act.Fori(0, B) as b:
                gate(b, bass.ds(b * SEQ, SEQ), 128, TILES)
            gate(B, slice(CLS, COLS), B, 1)

            def gelu(b, n):
                act.wait_ge(hid_done, b * HT + n + 1)
                act.wait_ge(hid_used, b * HT + n + 1)
                nc.scalar.activation(hid[:, n % HID_RING, :], banks(2 * (n % 2), 2), ACT.Gelu,
                                     bias=b1_sb[:, n:n + 1], scale=1.0 / WSCALE).then_inc(gelu_done, 1)

            act.wait_ge(hcls_biased, 1)
            nc.scalar.activation(hcls[:, :, :], hcls[:, :, :], ACT.Gelu).then_inc(hcls_gelu, 1)
            act.sem_inc(gelu_done, 2)
            with act.Fori(0, B) as b:
                for n in range(HT):
                    gelu(b, n)
            act.wait_ge(ocls_step, 3)
            act.dma_start(out[:, 0, :], h_tok[0:B, B * TILES, :]).then_inc(stored, 16)

        @block.vector
        def _(dve):
            dve.wait_ge(ident_landed, 16)
            nc.vector.tensor_copy(ident16[:, :], ident32[:, :]).then_inc(ident16_set, 1)
            nc.vector.tensor_tensor(fold[:, :], ident32[:, 0:D], ident32[:, D:2 * D], ALU.add).then_inc(ident16_set, 1)
            nc.vector.memset(xT[D:D + 1, :], 1.0).then_inc(ones_set, 1)
            nc.vector.memset(QA[64:96, :], 0.0).then_inc(ones_set, 1)
            nc.vector.memset(Vt[:, :, D:D + 1], 1.0).then_inc(ones_set, 1)
            dve.wait_ge(emb_w_summed, 1)
            nc.vector.tensor_copy(G[:, :, :, :], ps[:, 0, :].rearrange("p (o a q) -> p q a o", a=2, q=4)).then_inc(emb_w_ready, 1)
            dve.wait_ge(aug_landed, 48)
            nc.vector.tensor_scalar(qtab_sb[96:128, :], qtab_sb[96:128, :], qcol[96:128, 0:1], None, ALU.mult).then_inc(qaug_scaled, 1)
            dve.wait_ge(qaug_scaled, 1)
            nc.vector.tensor_copy(qhi[96:128, :], qtab_sb[96:128, :]).then_inc(qaug_split, 1)
            dve.wait_ge(qaug_split, 1)
            nc.vector.scalar_tensor_tensor(QA[96:128, 0:SEQ], qhi[96:128, 0:SEQ], qcol[96:128, 1:2],
                                           qtab_sb[96:128, 0:SEQ], ALU.mult, ALU.add).then_inc(qaug_ready, 1)
            nc.vector.scalar_tensor_tensor(QA[96:128, CLS:COLS], qhi[96:128, SEQ:SEQ + B], qcol[96:128, 1:2],
                                           qtab_sb[96:128, SEQ:SEQ + B], ALU.mult, ALU.add).then_inc(qaug_ready, 1)
            dve.wait_ge(qaug_ready, 1)
            for b in range(1, B):
                nc.vector.tensor_copy(QA[96:128, b * SEQ:(b + 1) * SEQ], QA[96:128, 0:SEQ]).then_inc(qaug_ready, 1)

            def spread(a, shape):
                return a.unsqueeze(2).broadcast_to(shape)

            def norm(k, src, rows, tiles, twice):
                r, s = slice(0, rows), slice(0, tiles)
                shape = [rows, tiles, D]
                nc.vector.tensor_reduce(stats[r, 0, s], src, AX_X, ALU.add).then_inc(ln_sum, 1)
                dve.wait_ge(ln_sum, k + 1)
                nc.vector.tensor_scalar(stats[r, 1, s], stats[r, 0, s], 1.0 / D, None, ALU.mult).then_inc(ln_mean, 1)
                dve.wait_ge(ln_mean, k + 1)
                nc.vector.tensor_tensor(centred[r, s, :], src, spread(stats[r, 1, s], shape), ALU.subtract).then_inc(ln_centred, 1)
                dve.wait_ge(ln_squared, k + 1)
                nc.vector.tensor_reduce(stats[r, 2, s], squares[r, s, :], AX_X, ALU.add).then_inc(ln_sumsq, 1)
                dve.wait_ge(ln_sumsq, k + 1)
                nc.vector.tensor_scalar(stats[r, 3, s], stats[r, 2, s], 1.0 / D, EPS, ALU.mult, ALU.add).then_inc(ln_var, 1)
                dve.wait_ge(ln_rstd, k + 1)
                for g in range(2 if twice else 1):
                    nc.vector.tensor_tensor(normed[r, s, g, :], centred[r, s, :], spread(stats[r, 4, s], shape),
                                            ALU.mult).then_inc(ln_done, 1)

            def project(k, cols, tiles, n, rows):
                dve.wait_ge(norm_T, k + 1)
                nc.vector.tensor_copy(xT[0:D, 0:n], banks(4, 2)[0:D, 0:n]).then_inc(xT_copied, 1)
                dve.wait_ge(q_hi, k + 1)
                nc.vector.scalar_tensor_tensor(QB[64:128, cols], banks(6, 2)[64:128, 0:n], QSCALE, QB[64:128, cols],
                                               ALU.mult, ALU.subtract).then_inc(q_lo, 1)
                dve.wait_ge(k_hi_again, k + 1)
                nc.vector.tensor_tensor(KB[0:64, cols], banks(4, 2)[0:64, 0:n], KA[0:64, cols], ALU.subtract).then_inc(k_lo, 1)
                dve.wait_ge(v_done, k + 1)
                nc.vector.tensor_copy(Vt[0:rows, tiles, 0:D], ps[0:rows, 3, 0:D * (n // rows)].rearrange("p (t d) -> p t d", d=D)).then_inc(v_copied, 1)

            with dve.Fori(0, B) as b:
                dve.wait_ge(tok_done, b + 1)
                tokens = h_tok[:, bass.ds(b * TILES, TILES), :]
                nc.vector.tensor_copy(tokens, ps[:, 3, :].rearrange("p (t d) -> p t d", d=D)).then_inc(tok_copied, 1)
                apart(dve)
                dve.wait_ge(tok_copied, b + 1)
                norm(b, tokens, 128, TILES, False)
                project(b, bass.ds(b * SEQ, SEQ), bass.ds(b * TILES, TILES), SEQ, 128)
            dve.wait_ge(cls_landed, 16)
            norm(B, h_tok[0:B, B * TILES:B * TILES + 1, :], B, 1, False)
            project(B, slice(CLS, COLS), slice(B * TILES, B * TILES + 1), B, B)
            dve.wait_ge(w1_hi, 2)
            nc.vector.scalar_tensor_tensor(WB[:, :], w1f[:, :], WSCALE, WA[:, :], ALU.mult, ALU.subtract).then_inc(w1_lo, 1)
            nc.vector.scalar_tensor_tensor(GB[:, :], wgf[:, :], WSCALE, GA[:, :], ALU.mult, ALU.subtract).then_inc(w1_lo, 1)

            def maxima(b):
                if not isinstance(b, int):
                    dve.wait_ge(mcls_ready, b)
                dve.wait_ge(side_full[0], side(b, 0, 0))
                nc.vector.tensor_copy(mpart[:, :, 2], ps[:, 6, 0:TILES]).then_inc(mcls_max, 1)
                nc.vector.tensor_copy(mcls[:, 2:3], ps[0:1, 6, TILES:TILES + 1]).then_inc(side_free[0], 1)
                for k in range(2):
                    dve.wait_ge(side_full[k], side(b, 1, k))
                    nc.vector.tensor_reduce(mcls[:, k:k + 1], ps[0:1, 6 + k, :], AX_X, ALU.max).then_inc(side_free[k], 1)
                for i in range(TILES):
                    for k in range(2):
                        dve.wait_ge(side_full[k], side(b, 2 + i, k))
                        nc.vector.tensor_reduce(mpart[:, i, k:k + 1], ps[:, 6 + k, :], AX_X, ALU.max).then_inc(side_free[k], 1)
                for k in range(2):
                    dve.wait_ge(side_free[k], side(b, 9, k))
                nc.vector.tensor_reduce(mneg[:, :], mpart[:, :, :], AX_X, ALU.max, negate=True).then_inc(m_ready, 1)
                nc.vector.tensor_reduce(QA[64:65, bass.ds(CLS + b, 1)], mcls[:, 0:3], AX_X, ALU.max, negate=True).then_inc(mcls_ready, 1)

            def normalise(b):
                sums = ps[:, 4:6, 0:4 * (D + 1)].rearrange("p a (i d) -> p a i d", d=D + 1)
                dve.wait_ge(acc_done, b + 2)
                nc.vector.reciprocal(rden[:, :].rearrange("p (a i) -> p a i", a=2), sums[:, :, :, D]).then_inc(acc_recip, 1)
                dve.wait_ge(acc_recip, b + 1)
                dve.wait_ge(attn_added, b + 1)
                r = rden[:, :].rearrange("p (a i) -> p a i", a=2).unsqueeze(3).broadcast_to([128, 2, 4, D])
                nc.vector.tensor_tensor(attn[:, :, :].rearrange("p (a i) d -> p a i d", a=2), sums[:, :, :, 0:D], r, ALU.mult).then_inc(acc_free, 1)

            dve.sem_inc(acc_free, 1)
            maxima(0)
            with dve.Fori(0, B - 1) as b:
                maxima(b + 1)
                normalise(b)
            normalise(B - 1)
            dve.wait_ge(cq_acc, 1)
            dve.wait_ge(acc_free, B + 1)
            nc.vector.reciprocal(rden[0:B, 0:1], ps[0:B, 7, D:D + 1]).then_inc(acc_recip, 1)
            dve.wait_ge(acc_recip, B + 1)
            dve.wait_ge(attn_added, B + 1)
            nc.vector.tensor_scalar(attn[0:B, 0, :], ps[0:B, 7, 0:D], rden[0:B, 0:1], None, ALU.mult).then_inc(acc_free, 1)

            def gate(k, cols, tiles, rows, n):
                r, s = slice(0, rows), slice(0, n)
                tokens = h_tok[r, tiles, :]
                norm(B + 1 + k, tokens, rows, n, True)
                dve.wait_ge(f_hi, k + 1)
                nc.vector.tensor_tensor(FA[64:128, cols], banks(0, 2)[64:128, 0:n * rows], FA[64:128, cols], ALU.subtract).then_inc(f_lo, 1)
                step = [GATE_STEPS * k]

                def done(ins):
                    step[0] = step[0] + 1
                    ins.then_inc(gate_step, 1)
                    dve.wait_ge(gate_step, step[0])

                dve.wait_ge(gate_done, k + 1)
                lg = logits[r, s, :]
                done(nc.vector.scalar_tensor_tensor(lg, ps[r, 2, 0:E * n].rearrange("p (t e) -> p t e", e=E), 1.0 / WSCALE,
                                                    bg_sb[r, :].unsqueeze(1).broadcast_to([rows, n, E]), ALU.mult, ALU.add))
                done(nc.vector.tensor_reduce(top[r, s], lg, AX_X, ALU.max))
                done(nc.vector.tensor_tensor(chosen[r, s, :], lg, top[r, s].unsqueeze(2).broadcast_to([rows, n, E]), ALU.subtract))
                done(nc.vector.tensor_tensor(diff[r, s, :, :], lg.unsqueeze(2).broadcast_to([rows, n, E, E]),
                                             lg.unsqueeze(3).broadcast_to([rows, n, E, E]), ALU.subtract))
                flat = lambda t: t[r, s, :, :].rearrange("p t e f -> p t (e f)")
                done(nc.vector.scalar_tensor_tensor(flat(equal), flat(diff), 0.0, before_sb[r, :].unsqueeze(1).broadcast_to([rows, n, E * E]),
                                                    ALU.is_equal, ALU.mult))
                done(nc.vector.scalar_tensor_tensor(flat(diff), flat(diff), 0.0, flat(equal), ALU.is_gt, ALU.add))
                done(nc.vector.tensor_reduce(rank[r, s, :], diff[r, s, :, :], AX_X, ALU.add))
                dve.wait_ge(gate_exp, k + 1)
                done(nc.vector.scalar_tensor_tensor(chosen[r, s, :], rank[r, s, :], 2.0, expd[r, s, :], ALU.is_lt, ALU.mult))
                done(nc.vector.tensor_reduce(csum[r, 0, s], chosen[r, s, :], AX_X, ALU.add))
                done(nc.vector.reciprocal(csum[r, 1, s], csum[r, 0, s]))
                dve.wait_ge(wtok_copied, k + 1)
                nc.vector.tensor_tensor(wcur[r, s, :], chosen[r, s, :], csum[r, 1, s].unsqueeze(2).broadcast_to([rows, n, E]),
                                        ALU.mult).then_inc(w_ready, 1)
                dve.wait_ge(wT_done, k + 1)
                nc.vector.tensor_copy(wT[:, 0:n * rows], banks(4, 2)[0:E, 0:n * rows]).then_inc(wT_copied, 1)
                dve.wait_ge(b2_done, k + 1)
                nc.vector.tensor_tensor(tokens, ps[r, 3, 0:D * n].rearrange("p (t d) -> p t d", d=D), tokens, ALU.add).then_inc(b2_added, 1)

            dve.wait_ge(attn_added, B + 2)
            with dve.Fori(0, B) as b:
                gate(b, bass.ds(b * SEQ, SEQ), bass.ds(b * TILES, TILES), 128, TILES)
            gate(B, slice(CLS, COLS), slice(B * TILES, B * TILES + 1), B, 1)

            dve.wait_ge(wtok_copied, B + 2)
            dve.wait_ge(hcls_done, 1)
            nc.vector.scalar_tensor_tensor(hcls[:, :, :], ps[:, 6, 0:HT * B].rearrange("p (n c) -> p n c", c=B), 1.0 / WSCALE,
                                           b1_sb[:, :].unsqueeze(2).broadcast_to([128, HT, B]), ALU.mult, ALU.add).then_inc(hcls_biased, 1)
            dve.wait_ge(ocls_done, 1)
            nc.vector.tensor_tensor(ocls[:, :, :], ps[0:B, 7, :].rearrange("p (e d) -> p e d", d=D),
                                    wtok[0:B, B * TILES, :].unsqueeze(2).broadcast_to([B, E, D]), ALU.mult).then_inc(ocls_step, 1)
            dve.wait_ge(ocls_step, 1)
            nc.vector.tensor_reduce(scls[:, :], ocls[:, :, :].rearrange("p e d -> p d e"), AX_X, ALU.add).then_inc(ocls_step, 1)
            dve.wait_ge(ocls_step, 2)
            nc.vector.tensor_tensor(h_tok[0:B, B * TILES, :], h_tok[0:B, B * TILES, :], scls[:, :], ALU.add).then_inc(ocls_step, 1)
            dve.sem_inc(out_weighed, OUT_RING)
            dve.sem_inc(out_added, OUT_RING)
            with dve.Fori(0, B) as b:
                tokens = h_tok[:, bass.ds(b * TILES, TILES), :]
                for e in range(E + 1):
                    if e < E:
                        dve.wait_ge(hid_used, b * HT + 2 * e + 2 + HID_RING)
                        dve.wait_ge(out_added, b * E + e + 1)
                        nc.vector.tensor_tensor(wout[:, e % 2, :, :], ps[:, 4 + e % 2, :].rearrange("p (t d) -> p t d", d=D),
                                                wtok[:, bass.ds(b * TILES, TILES), e].unsqueeze(2).broadcast_to([128, TILES, D]),
                                                ALU.mult).then_inc(out_weighed, 1)
                    if e > 0:
                        dve.wait_ge(out_weighed, b * E + e + OUT_RING)
                        dve.wait_ge(out_added, b * E + e + 1)
                        nc.vector.tensor_tensor(tokens, tokens, wout[:, (e - 1) % 2, :, :], ALU.add).then_inc(out_added, 1)

        @block.gpsimd
        def _(pool):
            nc.gpsimd.memset(half[:, :], -0.5).then_inc(consts_set, 1)
            nc.gpsimd.memset(Pz[:, :], 0.0).then_inc(consts_set, 1)
            nc.gpsimd.memset(normed[:, :, 1, :], 0.0).then_inc(ones_set, 1)
            nc.gpsimd.memset(FA[:, COLS:CLS + SEQ], 0.0).then_inc(ones_set, 1)

            def rstd(k, rows, tiles):
                pool.wait_ge(ln_var, k + 1)
                r, s = slice(0, rows), slice(0, tiles)
                nc.gpsimd.tensor_tensor(stats[r, 4, s], stats[r, 3, s], half[r, s], ALU.pow).then_inc(ln_rstd, 1)

            def high_again(k, cols):
                pool.wait_ge(q_hi, k + 1)
                nc.gpsimd.tensor_copy(QA[0:64, cols], QB[0:64, cols]).then_inc(q_hi_again, 1)
                pool.wait_ge(k_hi, k + 1)
                nc.gpsimd.tensor_copy(KA[0:64, cols], KB[0:64, cols]).then_inc(k_hi_again, 1)

            pool.wait_ge(consts_set, 2)
            with pool.Fori(0, B) as b:
                rstd(b, 128, TILES)
                high_again(b, bass.ds(b * SEQ, SEQ))
            rstd(B, B, 1)
            high_again(B, slice(CLS, COLS))

            pool.sem_inc(attn_added, 1)
            with pool.Fori(0, B) as b:
                apart(pool)
                pool.wait_ge(acc_free, b + 2)
                tokens = h_tok[:, bass.ds(b * TILES, TILES), :]
                nc.gpsimd.tensor_tensor(tokens, tokens, attn[:, :, :], ALU.add).then_inc(attn_added, 1)
            pool.wait_ge(acc_free, B + 2)
            tokens = h_tok[0:B, B * TILES, :]
            nc.gpsimd.tensor_tensor(tokens, tokens, attn[0:B, 0, :], ALU.add).then_inc(attn_added, 1)

            def keep_weights(k, tiles, rows, n):
                pool.wait_ge(w_ready, k + 1)
                nc.gpsimd.tensor_copy(wtok[0:rows, tiles, :], wcur[0:rows, 0:n, :]).then_inc(wtok_copied, 1)

            pool.sem_inc(wtok_copied, 1)
            with pool.Fori(0, B) as b:
                rstd(b + B + 1, 128, TILES)
                keep_weights(b, bass.ds(b * TILES, TILES), 128, TILES)
            rstd(2 * B + 1, B, 1)
            keep_weights(B, slice(B * TILES, B * TILES + 1), B, 1)

        @block.tensor
        def _(pe):
            pe.wait_ge(emb_w_landed, 32)
            for o in range(64):
                for h in range(2):
                    last = nc.tensor.matmul(ps[64 * h:64 * h + 64, 0, 8 * o:8 * o + 8], wf_sb[:, 64 * o:64 * o + 64],
                                            dft_sb[:, 8 * h:8 * h + 8], start=True, stop=True)
            last.then_inc(emb_w_summed, 1)

            def embed(b, first):
                pe.wait_ge(x_ready, b + 1)
                if not first:
                    pe.wait_ge(parts_copied, 2 * b)
                blocks = xs[:, bass.ds(b * XB, XB)].rearrange("p (j q v) -> p j q v", q=4, v=V)
                for c, j0 in enumerate(range(0, NBLK, 8)):
                    j1 = min(j0 + 8, NBLK)
                    for q in range(4):
                        last = nc.tensor.matmul(ps[:, c, 0:V * (j1 - j0)], G[:, q, :, :].rearrange("p a o -> p (a o)"),
                                                blocks[:, j0:j1, q, :], start=(q == 0), stop=(q == 3))
                last.then_inc(emb_done, 1)

            def tokens_of(b, first):
                pe.wait_ge(parts_copied, 2 * (b + 1))
                if not first:
                    pe.wait_ge(v_copied, b)
                for i in range(TILES):
                    last = nc.tensor.matmul(ps[:, 3, D * i:D * i + D], parts[:, 128 * i:128 * i + 128], fold[:, :], start=True, stop=True)
                last.then_inc(tok_done, 1)

            def projections(k, tiles, rows, first):
                pe.wait_ge(ln_done, k + 1)
                if not first:
                    pe.wait_ge(k_lo, k)
                for i in range(tiles):
                    last = nc.tensor.transpose(banks(4, 2)[:, 128 * i:128 * i + rows], normed[0:rows, i, :, :].rearrange("p g d -> p (g d)"), ident32[0:rows, 0:rows])
                last.then_inc(norm_T, 1)
                n = rows * tiles
                pe.wait_ge(xT_copied, k + 1)
                if not first:
                    pe.wait_ge(q_lo, k)
                for w, bank, full in ((wq_sb, 6, q_done), (wk_sb, 4, k_done)):
                    for c in range(0, n, 512):
                        m = min(512, n - c)
                        last = nc.tensor.matmul(ps[:, bank + c // 512, 0:m], w[:, :], xT[:, c:c + m], start=True, stop=True)
                    last.then_inc(full, 1)
                for i in range(tiles):
                    last = nc.tensor.matmul(ps[0:rows, 3, D * i:D * i + D], xT[:, i * 128:i * 128 + rows], wv_sb[:, :], start=True, stop=True)
                last.then_inc(v_done, 1)

            pe.wait_ge(emb_w_ready, 1)
            embed(0, True)
            pe.wait_ge(ident_landed, 16)
            pe.wait_ge(ident16_set, 2)
            tokens_of(0, True)
            pe.wait_ge(proj_w_landed, 48)
            pe.wait_ge(ones_set, 5)
            embed(1, False)
            projections(0, TILES, 128, True)
            with pe.Fori(1, B - 1) as b:
                tokens_of(b, False)
                embed(b + 1, False)
                projections(b, TILES, 128, False)
            tokens_of(B - 1, False)
            projections(B - 1, TILES, 128, False)
            pe.wait_ge(v_copied, B)
            projections(B, 1, B, False)

            def cols(b, t, n):
                return bass.ds(b * SEQ + t, n)

            def own(b, turn, bank):
                before_it = side(b, turn, bank) - 1
                if not (isinstance(before_it, int) and before_it == 0):
                    pe.wait_ge(side_free[bank], before_it)

            def turn(b, n):
                if n == 0:
                    own(b, n, 0)
                    for i in range(TILES):
                        nc.tensor.matmul(ps[:, 6, i:i + 1], QA[:, cols(b, 128 * i, 128)], KA[:, CLS:CLS + 1], start=True, stop=True)
                    nc.tensor.matmul(ps[0:1, 6, TILES:TILES + 1], QA[:, COLS - 1:COLS], KA[:, CLS:CLS + 1],
                                     start=True, stop=True).then_inc(side_full[0], 1)
                elif n == 1:
                    for k in range(2):
                        own(b, n, k)
                        nc.tensor.matmul(ps[0:1, 6 + k, :], QA[:, COLS - 1:COLS], KA[:, cols(b, 512 * k, 512)],
                                         start=True, stop=True).then_inc(side_full[k], 1)
                elif n < 10:
                    for k in range(2):
                        own(b, n, k)
                        nc.tensor.matmul(ps[:, 6 + k, :], QA[:, cols(b, 128 * (n - 2), 128)], KA[:, cols(b, 512 * k, 512)],
                                         start=True, stop=True).then_inc(side_full[k], 1)
                elif n == 10:
                    pe.wait_ge(m_ready, b + 1)
                    for k in range(2):
                        own(b, n, k)
                        for i in range(4):
                            last = nc.tensor.matmul(ps[64:65, 6 + k, 128 * i:128 * i + 128], mneg[:, 4 * k + i:4 * k + i + 1],
                                                    ident16[:, :], start=True, stop=True)
                        last.then_inc(side_full[k], 1)
                else:
                    for k in range(2):
                        own(b, n, k)
                    for k in range(2):
                        for g, (KX, QX) in enumerate(((KA, QA), (KB, QB))):
                            last = nc.tensor.matmul(ps[0:1, 6 + k, :], KX[:, CLS:CLS + 1], QX[:, cols(b, 512 * k, 512)],
                                                    start=(g == 0), stop=(g == 1))
                        last.then_inc(side_full[k], 1)

            def scores(b, t):
                pe.wait_ge(exp_done, b * TILES + t + 1)
                pair = 2 * (t % 2)
                for g, (KX, QX) in enumerate(((KA, QA), (KB, QB))):
                    for k in range(2):
                        last = nc.tensor.matmul(ps[:, pair + k, :], KX[:, cols(b, 128 * t, 128)], QX[:, cols(b, 512 * k, 512)],
                                                start=(g == 0), stop=(g == 1))
                last.then_inc(score_done, 1)

            def sum_tile(i):
                return ps[:, 4 + i // 4, (D + 1) * (i % 4):(D + 1) * (i % 4 + 1)]

            def values(b, t):
                pe.wait_ge(exp_done, b * TILES + t + 1 + SCORE_RING)
                if t == 0:
                    pe.wait_ge(acc_free, b + 1)
                for i in range(TILES):
                    last = nc.tensor.matmul(sum_tile(i), P[:, t % P_RING, 128 * i:128 * i + 128], Vt[:, bass.ds(b * TILES + t, 1), :],
                                            start=(t == 0 and i % 4 == 0), stop=False, skip_group_check=True)
                last.then_inc(pv_done, 1)

            def class_values(b):
                for k in range(2):
                    pe.wait_ge(side_free[k], side(b, 11, k))
                for i in range(TILES):
                    last = nc.tensor.matmul(sum_tile(i), Pc[:, 128 * i:128 * i + 128], Vt[0:1, B * TILES, :],
                                            start=False, stop=True, skip_group_check=True)
                last.then_inc(acc_done, 1)

            def attend(b, more):
                turn(b, 11)
                scores(b, 0)
                scores(b, 1)
                for t in range(TILES):
                    values(b, t)
                    if t + 2 < TILES:
                        scores(b, t + 2)
                    if more:
                        for n in TURNS[t]:
                            turn(b + 1, n)
                class_values(b)

            TURNS = [[0, 1], [2, 3], [4, 5], [6, 7], [8, 9], [], [10], []]
            pe.sem_inc(pv_done, P_RING)
            pe.sem_inc(acc_done, 1)
            pe.wait_ge(q_lo, B + 1)
            pe.wait_ge(k_lo, B + 1)
            pe.wait_ge(q_hi_again, B + 1)
            pe.wait_ge(v_copied, B + 1)
            pe.wait_ge(qaug_ready, B + 1)
            pe.wait_ge(ktab_landed, 16 * (B + 1))
            for n in range(11):
                turn(0, n)
            with pe.Fori(0, B - 1) as b:
                attend(b, True)
            attend(B - 1, False)

            pe.wait_ge(mcls_ready, B)
            pe.wait_ge(side_free[0], B * USES[0])
            with pe.Fori(0, B) as b:
                for t in range(TILES):
                    for g, (KX, QX) in enumerate(((KA, QA), (KB, QB))):
                        nc.tensor.matmul(ps[:, 6, bass.ds(b * TILES + t, 1)], KX[:, cols(b, 128 * t, 128)], QX[:, bass.ds(CLS + b, 1)],
                                         start=(g == 0), stop=(g == 1))
            for g, (KX, QX) in enumerate(((KA, QA), (KB, QB))):
                last = nc.tensor.matmul(ps[0:1, 6, B * TILES:B * TILES + B], KX[:, CLS:CLS + 1], QX[:, CLS:COLS], start=(g == 0), stop=(g == 1))
            last.then_inc(cq_scored, 1)
            pe.wait_ge(cq_exp, 2)
            pe.wait_ge(side_free[1], B * USES[1])
            for u in range(B * TILES):
                bb, t = divmod(u, TILES)
                nc.tensor.matmul(ps[0:B, 7, 0:D + 1], Pz[:, 33 * bb + 4 * t - bb:33 * bb + 4 * t - bb + B], Vt[:, u, :],
                                 start=(u == 0), stop=False)
            nc.tensor.matmul(ps[0:B, 7, 0:D + 1], Pzc[:, :], Vt[0:1, B * TILES, :], start=False, stop=True).then_inc(cq_acc, 1)

            def gate(k, tiles, rows, col):
                pe.wait_ge(ln_done, B + 1 + 2 * (k + 1))
                for i in range(tiles):
                    last = nc.tensor.transpose(banks(0, 2)[:, 128 * i:128 * i + rows],
                                               normed[0:rows, i, :, :].rearrange("p g d -> p (g d)"), ident32[0:rows, 0:rows])
                last.then_inc(norm_T, 1)
                pe.wait_ge(f_lo, k + 1)
                for i in range(tiles):
                    for g, W in enumerate((GA, GB)):
                        last = nc.tensor.matmul(ps[0:rows, 2, E * i:E * i + E], FA[:, bass.ds(col + 128 * i, rows) if tiles > 1 else slice(CLS, COLS)], W[:, :],
                                                start=(g == 0), stop=(g == 1))
                last.then_inc(gate_done, 1)
                pe.wait_ge(w_ready, k + 1)
                for i in range(tiles):
                    last = nc.tensor.transpose(banks(4, 2)[0:E, 128 * i:128 * i + rows], wcur[0:rows, i, :], ident32[0:rows, 0:rows])
                last.then_inc(wT_done, 1)
                pe.wait_ge(wT_copied, k + 1)
                for i in range(tiles):
                    last = nc.tensor.matmul(ps[0:rows, 3, D * i:D * i + D], wT[:, 128 * i:128 * i + rows], b2_sb[:, :], start=True, stop=True)
                last.then_inc(b2_done, 1)

            pe.wait_ge(acc_free, B + 1)
            pe.wait_ge(w1_lo, 2)
            with pe.Fori(0, B) as b:
                gate(b, TILES, 128, b * SEQ)
            gate(B, 1, B, CLS)

            def hidden(b, n):
                pe.wait_ge(gelu_done, b * HT + n + 1)
                for g, W in enumerate((WA, WB)):
                    for k in range(2):
                        last = nc.tensor.matmul(ps[:, 2 * (n % 2) + k, :], W[:, 128 * n:128 * n + 128], FA[:, cols(b, 512 * k, 512)],
                                                start=(g == 0), stop=(g == 1))
                last.then_inc(hid_done, 1)

            def expert_out(b, n):
                e, j = divmod(n, 2)
                pe.wait_ge(gelu_done, b * HT + n + 1 + 2)
                if j == 0:
                    pe.wait_ge(out_weighed, b * E + e + 1)
                for i in range(TILES):
                    last = nc.tensor.matmul(ps[:, 4 + e % 2, D * i:D * i + D], hid[:, n % HID_RING, 128 * i:128 * i + 128], w2_sb[:, n, :],
                                            start=(j == 0 and i == 0), stop=(j == 1), skip_group_check=True)
                last.then_inc(hid_used, 1)

            for n in range(HT):
                for g, W in enumerate((WA, WB)):
                    last = nc.tensor.matmul(ps[:, 6, B * n:B * n + B], W[:, 128 * n:128 * n + 128], FA[:, CLS:COLS], start=(g == 0), stop=(g == 1))
            last.then_inc(hcls_done, 1)
            pe.wait_ge(hcls_gelu, 1)
            for e in range(E):
                for j in range(2):
                    last = nc.tensor.matmul(ps[0:B, 7, D * e:D * e + D], hcls[:, 2 * e + j, :], w2_sb[:, 2 * e + j, :], start=(j == 0), stop=(j == 1))
            last.then_inc(ocls_done, 1)

            pe.sem_inc(hid_used, HID_RING)
            pe.wait_ge(b2_added, B + 1)
            hidden(0, 0)
            with pe.Fori(0, B) as b:
                for n in range(HT):
                    if n + 1 < HT:
                        hidden(b, n + 1)
                    else:
                        hidden(b + 1, 0)
                    expert_out(b, n)


def _tables():
    f, p = np.arange(PATCH // 2 + 1)[:, None], np.arange(PATCH)[None, :]
    angle = 2 * np.pi * f * p / PATCH
    by_step = np.concatenate([np.cos(angle), -np.sin(angle)]) / np.sqrt(PATCH)
    dft = by_step.reshape(NF, 2, 2, 4).transpose(0, 2, 1, 3).reshape(NF, PATCH)
    pos = np.concatenate([np.arange(1, SEQ + 1), np.zeros(B)])
    trig = np.stack([g(2 * np.pi * pos / period) for period in PERIODS for g in (np.cos, np.sin)])
    hi = trig.astype(np.float16)
    lo = (trig - hi).astype(np.float16)
    qtab = np.zeros((32, SEQ + B), np.float32)
    qtab[0:12] = np.tile(trig, (3, 1))
    negmask = np.zeros((32, 1), np.float32)
    negmask[8:12] = -1
    ktab = np.zeros((64, SEQ + B), np.float16)
    ktab[0] = 1
    ktab[32:44] = np.concatenate([hi, lo, hi])
    before = (np.arange(E)[None, :] < np.arange(E)[:, None]).astype(np.float32).reshape(1, E * E)
    return {"dft": dft.astype(np.float32), "ident": np.eye(128, dtype=np.float32), "qtab": qtab, "ktab": ktab,
            "negmask": negmask, "before": before}


def kernel(x, cls_tok, L0_tok_W, L0_attn_Wq, L0_attn_bq, L0_attn_Wk, L0_attn_bk, L0_attn_Wv, L0_attn_bv, L0_attn_beta,
           L0_ffn_Wg, L0_ffn_bg, L0_ffn_W1, L0_ffn_b1, L0_ffn_W2, L0_ffn_b2):
    import concourse.bacc as bacc
    from concourse.bass_utils import run_bass_kernel_spmd

    def with_bias(w, b, copies):
        w, b = np.asarray(w), np.asarray(b)
        return np.concatenate([np.concatenate([w.T, b[None, :]])] * copies, axis=1)

    beta = np.asarray(L0_attn_beta)
    zeros = np.zeros((20, 1), np.float32)
    arrays = {
        "x": x, "cls_tok": cls_tok,
        "wf": np.asarray(L0_tok_W).reshape(64, NF, C).transpose(1, 0, 2).reshape(NF, 64 * C),
        "wq": with_bias(L0_attn_Wq, L0_attn_bq, 2), "wk": with_bias(L0_attn_Wk, L0_attn_bk, 2),
        "wv": with_bias(L0_attn_Wv, L0_attn_bv, 1),
        "beta": np.concatenate([beta[[0, 0, 1, 1] * 3][:, None], zeros]),
        "wg": L0_ffn_Wg, "bg": L0_ffn_bg, "w1": L0_ffn_W1,
        "b1": np.asarray(L0_ffn_b1).reshape(HT, 128).T,
        "w2": L0_ffn_W2, "b2": L0_ffn_b2,
    }
    arrays.update(_tables())
    arrays = {k: np.ascontiguousarray(v) for k, v in arrays.items()}
    nc = bacc.Bacc("TRN2", target_bir_lowering=False, num_devices=1)
    aps = {k: nc.dram_tensor(f"{k}_dram", v.shape, mybir.dt.from_np(v.dtype), kind="ExternalInput").ap() for k, v in arrays.items()}
    out = nc.dram_tensor("out_dram", (B, SEQ + 1, D), F32, kind="ExternalOutput").ap()
    build(nc, out=out, **aps)
    r = run_bass_kernel_spmd(nc, [{f"{k}_dram": v for k, v in arrays.items()}], core_ids=[0])
    return r.results[0]["out_dram"]
```

```python
from contextlib import ExitStack

import numpy as np

import concourse.bass as bass
from concourse import mybir

F32 = mybir.dt.float32
F16 = mybir.dt.float16
ALU = mybir.AluOpType
ACT = mybir.ActivationFunctionType
AX_X = mybir.AxisListType.X

B, C, T, V = 4, 64, 128, 64
PATCH, STRIDE = 16, 8
NP = T // STRIDE
NBLK = NP + 1
NF = 2 * (PATCH // 2 + 1)
D = 64
SEQ = V * NP
TILES = SEQ // 128
ALL = B * TILES + 1
CLS = B * SEQ
COLS = CLS + B
E, H = 8, 256
HT = E * H // 128
EPS = 1e-5
WSCALE = 64.0
QSCALE = D ** -0.5
GATE_STEPS = 10
PERIODS = (24.0, 720.0)
XB = NBLK * 4 * V
OG = 128 // NF
OGROUPS = -(-64 // OG)
OBANK = 512 // (OG * PATCH)


def build(nc, x, cls_tok, wf, wqk, wv, beta, wg, bg, w1, b1, w2, b2,
          dft, ident, qtab, ktab, negmask, before, sel, out):
    ctx = ExitStack()
    with ctx:
        def sb(name, shape, dt=F32):
            return ctx.enter_context(nc.sbuf_tensor(name, shape, dt))

        def sem(name):
            return ctx.enter_context(nc.semaphore(name))

        xs = sb("xs", [128, B * XB])
        def later(first, n):
            assert first + n <= B * XB
            return xs[:, first:first + n]

        AD, AE = ALL * D, ALL * E * E
        P = later(0, 4 * SEQ).rearrange("p (r n) -> p r n", r=4)
        centred2 = later(0, AD).rearrange("p (t d) -> p t d", d=D)
        squares2 = later(AD + 5 * SEQ, AD).rearrange("p (t d) -> p t d", d=D)
        normed2 = later(2 * AD + 5 * SEQ, AD).rearrange("p (t d) -> p t d", d=D)
        wcur = later(AD, AD).rearrange("p (t g e) -> p t g e", g=2, e=32)
        diff = later(AD + 5 * SEQ, AE).rearrange("p (t e f) -> p t e f", e=E, f=E)
        equal = later(3 * AD + 5 * SEQ, AE).rearrange("p (t e f) -> p t e f", e=E, f=E)
        hid = later(2 * AD, 4 * SEQ).rearrange("p (r n) -> p r n", r=4)
        wspread = later(AD + 5 * SEQ + AE, 2 * SEQ).rearrange("p (r n) -> p r n", r=2)
        esum = later(0, SEQ)
        eterm = later(SEQ, SEQ)
        ident32 = sb("ident32", [128, 128])
        ident16 = sb("ident16", [128, 128], F16)
        wf_sb = sb("wf_sb", [OG * NF, OGROUPS, 128])
        dft_sb = sb("dft_sb", [OG * NF, OG * PATCH])
        G = sb("G", [128, 4, 2, 64])
        parts = sb("parts", [128, SEQ])
        fold = sb("fold", [128, D])
        wqk_sb = sb("wqk_sb", [D + 1, 128])
        wv_sb = sb("wv_sb", [D + 1, D])
        h_tok = sb("h_tok", [128, B * TILES + 1, D])
        centred = sb("centred", [128, TILES, D])
        squares = sb("squares", [128, TILES, D])
        normed = sb("normed", [128, TILES, 2, D])
        stats = sb("stats", [128, 5, TILES])
        half = sb("half", [128, TILES])
        stats2 = sb("stats2", [128, 5, ALL])
        xT = sb("xT", [D + 1, SEQ])
        QA = sb("QA", [128, COLS], F16)
        QB = sb("QB", [128, COLS], F16)
        KA = sb("KA", [128, COLS], F16)
        KB = sb("KB", [128, COLS], F16)
        qtab_sb = sb("qtab_sb", [128, SEQ + B])
        qhi = sb("qhi", [128, SEQ + B], F16)
        qcol = sb("qcol", [128, 2])
        Vt = sb("Vt", [128, B * TILES + 1, D + 1])
        Pc = sb("Pc", [1, SEQ])
        Pz = sb("Pz", [128, B * 33])
        Pzc = sb("Pzc", [1, B])
        mpart = sb("mpart", [128, TILES, 3])
        mneg = sb("mneg", [128, TILES], F16)
        mcls = sb("mcls", [1, 4])
        rden = sb("rden", [128, TILES])
        attn = sb("attn", [128, TILES, D])
        FA = sb("FA", [128, CLS + 512 * 2], F16)
        w1f = sb("w1f", [128, COLS // 2])
        WA = sb("WA", [128, E * H], F16)
        WB = sb("WB", [128, E * H], F16)
        w2_sb = sb("w2_sb", [128, HT, D])
        b1_sb = sb("b1_sb", [128, HT])
        wT = w1f[:, :].bitcast(F16)
        b2f = sb("b2f", [128, D])
        B2A = sb("B2A", [128, D], F16)
        B2B = sb("B2B", [128, D], F16)
        sel_sb = sb("sel_sb", [128, E // 2, 128], F16)
        wgf = sb("wgf", [128, E])
        GA = sb("GA", [128, E], F16)
        GB = sb("GB", [128, E], F16)
        bg_sb = sb("bg_sb", [128, E])
        before_sb = sb("before_sb", [128, E * E])
        logits = sb("logits", [128, ALL, E])
        rank = sb("rank", [128, ALL, E])
        top = sb("top", [128, ALL])
        expd = sb("expd", [128, ALL, E])
        chosen = sb("chosen", [128, ALL, E])
        csum = sb("csum", [128, 2, ALL])
        hcls = sb("hcls", [128, HT, B])
        ocls = sb("ocls", [B, E, D])
        scls = sb("scls", [B, D])

        ps = ctx.enter_context(nc.psum_tensor("ps", [128, 8, 512], F32))

        def banks(first, count=1):
            return ps[:, first:first + count, :].rearrange("p b n -> p (b n)")

        x_landed = [sem(f"x_landed{b}") for b in range(B)]
        x_ready = sem("x_ready")
        emb_w_landed = sem("emb_w_landed")
        ident_landed = sem("ident_landed")
        proj_w_landed = sem("proj_w_landed")
        aug_landed = sem("aug_landed")
        ktab_landed = sem("ktab_landed")
        cls_landed = sem("cls_landed")
        ffn_w_landed = sem("ffn_w_landed")
        gate_w_landed = sem("gate_w_landed")
        stored = sem("stored")
        ones_set = sem("ones_set")
        consts_set = sem("consts_set")
        ident16_set = sem("ident16_set")
        emb_w_summed = sem("emb_w_summed")
        emb_w_ready = sem("emb_w_ready")
        qaug_scaled = sem("qaug_scaled")
        qaug_split = sem("qaug_split")
        qaug_ready = sem("qaug_ready")
        w1_hi = sem("w1_hi")
        w1_lo = sem("w1_lo")
        emb_done = sem("emb_done")
        parts_copied = sem("parts_copied")
        tok_done = sem("tok_done")
        tok_copied = sem("tok_copied")
        ln_sum = sem("ln_sum")
        ln_mean = sem("ln_mean")
        ln_centred = sem("ln_centred")
        ln_squared = sem("ln_squared")
        ln_sumsq = sem("ln_sumsq")
        ln_var = sem("ln_var")
        ln_rstd = sem("ln_rstd")
        ln_done = sem("ln_done")
        norm_T = sem("norm_T")
        xT_copied = sem("xT_copied")
        qk_done = sem("qk_done")
        hi_again = sem("hi_again")
        q_hi = sem("q_hi")
        q_lo = sem("q_lo")
        k_hi = sem("k_hi")
        k_lo = sem("k_lo")
        v_done = sem("v_done")
        v_copied = sem("v_copied")
        side_full = [sem("side_full0"), sem("side_full1")]
        side_free = [sem("side_free0"), sem("side_free1")]
        m_ready = sem("m_ready")
        mcls_max = sem("mcls_max")
        mcls_ready = sem("mcls_ready")
        score_done = sem("score_done")
        exp_done = sem("exp_done")
        clskey_exp = sem("clskey_exp")
        pv_done = sem("pv_done")
        acc_done = sem("acc_done")
        acc_recip = sem("acc_recip")
        acc_free = sem("acc_free")
        attn_added = sem("attn_added")
        cq_scored = sem("cq_scored")
        cq_exp = sem("cq_exp")
        cq_acc = sem("cq_acc")
        clstok_cleared = sem("clstok_cleared")
        wcur_cleared = sem("wcur_cleared")
        wT_cleared = sem("wT_cleared")
        b2_cleared = sem("b2_cleared")
        b2_landed = sem("b2_landed")
        b2_hi = sem("b2_hi")
        b2_lo = sem("b2_lo")
        n2_T = sem("n2_T")
        f_hi = sem("f_hi")
        f_lo = sem("f_lo")
        gate_done = sem("gate_done")
        gate_step = sem("gate_step")
        gate_exp = sem("gate_exp")
        w_ready = sem("w_ready")
        wT_done = sem("wT_done")
        wT_hi = sem("wT_hi")
        wT_lo = sem("wT_lo")
        hid_done = sem("hid_done")
        gelu_done = sem("gelu_done")
        step_used = sem("step_used")
        pair_done = sem("pair_done")
        spread_done = sem("spread_done")
        spread_copied = sem("spread_copied")
        term_ready = sem("term_ready")
        sum_ready = sem("sum_ready")
        fold_done = sem("fold_done")
        tokens_done = sem("tokens_done")
        hcls_done = sem("hcls_done")
        hcls_biased = sem("hcls_biased")
        hcls_gelu = sem("hcls_gelu")
        ocls_done = sem("ocls_done")
        ocls_step = sem("ocls_step")

        P_RING, SCORE_RING = 4, 2

        USES = (12, 11)

        def side(b, n, bank):
            return b * USES[bank] + n + 1 - bank

        PAIRS = E // 2

        def tile_count(c):
            return TILES if c < B else 1

        def tiles_of(c):
            return slice(c * TILES, c * TILES + tile_count(c))

        def tokens_of(c):
            return slice(c * SEQ, c * SEQ + 128 * tile_count(c))

        def wT_count(c):
            return SEQ if c < B else B

        def wT_cols(c):
            return slice(c * SEQ, c * SEQ + wT_count(c))

        def norm_banks(c):
            return (2 * (c % 2), 2)

        def w_banks(c):
            return (6 - 2 * (c % 2), 2)

        def tile_at(x):
            return 2 * (2 * (x // 4) + x % 2) + x % 4 // 2

        def apart(engine):
            engine.wait_ge(consts_set, 2)

        block = ctx.enter_context(nc.Block())

        @block.sync
        def _(sp):
            sp.dma_start(wf_sb[:, :, :], wf.rearrange("p (r n) -> p r n", n=128)).then_inc(emb_w_landed, 16)
            sp.dma_start(dft_sb[:, :], dft).then_inc(emb_w_landed, 16)
            sp.dma_start(ident32[:, :], ident).then_inc(ident_landed, 16)
            for b in range(B):
                for h in range(2):
                    to = xs[64 * h:64 * h + 64, b * XB:(b + 1) * XB].rearrange("p (j n) -> p j n", n=4 * V)
                    src = x[b].rearrange("c (j h q) v -> h c j (q v)", h=2, q=4)[h]
                    sp.dma_start(to[:, 0:NP, :], src).then_inc(x_landed[b], 16)
                    pad = to[:, NP, :].rearrange("p (q v) -> p q v", q=4)
                    sp.dma_start(pad, x[b, :, T - 1:T, :].broadcast_to([C, 4, V])).then_inc(x_landed[b], 16)
            for b in range(B):
                sp.wait_ge(x_landed[b], 64)
                sp.sem_inc(x_ready, 1)
            with sp.Fori(0, B) as b:
                sp.wait_ge(tokens_done, b + 1)
                sp.dma_start(out[bass.ds(b, 1), 1:SEQ + 1, :].rearrange("a (i p) d -> p (a i) d", p=128),
                             h_tok[:, bass.ds(b * TILES, TILES), :]).then_inc(stored, 16)
            sp.wait_ge(stored, 16 * (B + 1))

        @block.scalar
        def _(act):
            act.dma_start(wqk_sb[:, :], wqk).then_inc(proj_w_landed, 16)
            act.dma_start(wv_sb[:, :], wv).then_inc(proj_w_landed, 16)
            act.dma_start(qtab_sb[96:128, :], qtab).then_inc(aug_landed, 16)
            act.dma_start(qcol[96:128, 0:1], beta).then_inc(aug_landed, 16)
            act.dma_start(qcol[96:128, 1:2], negmask).then_inc(aug_landed, 16)
            act.wait_ge(clstok_cleared, 1)
            act.dma_start(h_tok[0:B, B * TILES, :], cls_tok[0].broadcast_to([B, D])).then_inc(cls_landed, 16)
            for b in range(B):
                act.dma_start(KA[64:128, b * SEQ:(b + 1) * SEQ], ktab[:, 0:SEQ]).then_inc(ktab_landed, 16)
            act.dma_start(KA[64:128, CLS:COLS], ktab[:, SEQ:SEQ + B]).then_inc(ktab_landed, 16)
            w1_d = w1.rearrange("e d h -> d e h")
            for g in range(2):
                act.dma_start(w1f[64 * g:64 * g + 64, 0:E * H].rearrange("p (e h) -> p e h", e=E), w1_d).then_inc(ffn_w_landed, 16)
            act.dma_start(w2_sb[:, :, :], w2.rearrange("e (j p) d -> p (e j) d", p=128)).then_inc(ffn_w_landed, 16)
            act.dma_start(b1_sb[:, :], b1).then_inc(ffn_w_landed, 16)
            act.wait_ge(b2_cleared, 1)
            for g in range(2):
                act.dma_start(b2f[32 * g:32 * g + E, :], b2).then_inc(b2_landed, 16)
            act.dma_start(sel_sb[:, :, :], sel.rearrange("p (a m) -> p a m", m=128)).then_inc(ffn_w_landed, 16)
            for g in range(2):
                act.dma_start(wgf[64 * g:64 * g + 64, :], wg).then_inc(gate_w_landed, 16)
            act.dma_start(bg_sb[:, :], bg.rearrange("(a e) -> a e", a=1).broadcast_to([128, E])).then_inc(gate_w_landed, 16)
            act.dma_start(before_sb[:, :], before.broadcast_to([128, E * E])).then_inc(gate_w_landed, 16)

            def square(k, rows, tiles):
                act.wait_ge(ln_centred, k + 1)
                nc.scalar.activation(squares[0:rows, 0:tiles, :], centred[0:rows, 0:tiles, :], ACT.Square).then_inc(ln_squared, 1)

            def copy_parts(b, first):
                act.wait_ge(emb_done, b + 1)
                if not first:
                    act.wait_ge(tok_done, b)
                for a in range(2):
                    rows = slice(64 * a, 64 * a + 64)
                    by_patch = banks(0, 3)[rows, V * a:V * (a + NP)].rearrange("p (n v) -> p v n", v=V)
                    nc.scalar.activation(parts[rows, :].rearrange("p (v n) -> p v n", n=NP), by_patch, ACT.Copy).then_inc(parts_copied, 1)

            def project_hi(k, cols, n):
                act.wait_ge(qk_done, k + 1)
                nc.scalar.activation(QB[0:64, cols], banks(6, 2)[0:64, 0:n], ACT.Copy, scale=QSCALE).then_inc(q_hi, 1)
                nc.scalar.activation(KB[64:128, cols], banks(6, 2)[64:128, 0:n], ACT.Copy).then_inc(k_hi, 1)

            copy_parts(0, True)
            square(0, 128, TILES)
            copy_parts(1, False)
            with act.Fori(0, B - 2) as b:
                square(b + 1, 128, TILES)
                project_hi(b, bass.ds(b * SEQ, SEQ), SEQ)
                copy_parts(b + 2, False)
            square(B - 1, 128, TILES)
            project_hi(B - 2, slice((B - 2) * SEQ, (B - 1) * SEQ), SEQ)
            square(B, B, 1)
            project_hi(B - 1, slice((B - 1) * SEQ, B * SEQ), SEQ)
            project_hi(B, slice(CLS, COLS), B)
            act.wait_ge(ffn_w_landed, 80)
            nc.scalar.activation(WA[:, :], w1f[:, 0:E * H], ACT.Copy, scale=WSCALE).then_inc(w1_hi, 1)
            act.wait_ge(gate_w_landed, 64)
            nc.scalar.activation(GA[:, :], wgf[:, :], ACT.Copy, scale=WSCALE).then_inc(w1_hi, 1)
            act.wait_ge(b2_landed, 32)
            nc.scalar.activation(B2A[:, :], b2f[:, :], ACT.Copy).then_inc(b2_hi, 1)


            def row_of_maxima(b):
                for k in range(2):
                    act.wait_ge(side_full[k], side(b, 10, k))
                    nc.scalar.activation(QA[64:65, bass.ds(b * SEQ + 512 * k, 512)], ps[64:65, 6 + k, :],
                                         ACT.Copy).then_inc(side_free[k], 1)

            def exponentials(b):
                act.wait_ge(acc_done, b + 1)
                for k in range(2):
                    act.wait_ge(side_full[k], side(b, 11, k))
                    nc.scalar.activation(Pc[:, 512 * k:512 * k + 512], ps[0:1, 6 + k, :], ACT.Exp).then_inc(side_free[k], 1)
                for t in range(TILES):
                    act.wait_ge(score_done, b * TILES + t + 1)
                    act.wait_ge(pv_done, b * TILES + t + 1)
                    nc.scalar.activation(P[:, t % P_RING, :], banks(2 * (t % 2), 2), ACT.Exp).then_inc(exp_done, 1)

            act.sem_inc(exp_done, SCORE_RING)
            row_of_maxima(0)
            with act.Fori(0, B - 1) as b:
                exponentials(b)
                row_of_maxima(b + 1)
            exponentials(B - 1)
            act.wait_ge(consts_set, 2)
            act.wait_ge(cq_scored, 1)
            diagonal = Pz[:, :].rearrange("p (b r) -> p b r", b=B)[:, :, 0:4 * TILES:4]
            nc.scalar.activation(diagonal, ps[:, 6, 0:B * TILES].rearrange("p (b t) -> p b t", b=B), ACT.Exp).then_inc(cq_exp, 1)
            nc.scalar.activation(Pzc[:, :], ps[0:1, 6, B * TILES:B * TILES + B], ACT.Exp).then_inc(cq_exp, 1)

            for c in range(B + 1):
                act.wait_ge(ln_centred, B + 1 + c + 1)
                nc.scalar.activation(squares2[:, tiles_of(c), :], centred2[:, tiles_of(c), :], ACT.Square).then_inc(ln_squared, 1)
            for c in range(B + 1):
                act.wait_ge(n2_T, c + 1)
                nc.scalar.activation(FA[0:64, tokens_of(c)], banks(*norm_banks(c))[0:64, 0:128 * tile_count(c)], ACT.Copy).then_inc(f_hi, 1)
            act.wait_ge(gate_step, 3)
            nc.scalar.activation(expd[:, :, :], chosen[:, :, :], ACT.Exp).then_inc(gate_exp, 1)

            def gelu(b, x):
                n = tile_at(x)
                act.wait_ge(hid_done, b * HT + x + 1)
                if not (isinstance(b, int) and x < 4):
                    act.wait_ge(step_used, b * (HT // 2) + x // 2 - 1)
                nc.scalar.activation(hid[:, x % 4, :], banks(2 * (x % 2), 2), ACT.Gelu,
                                     bias=b1_sb[:, n:n + 1], scale=1.0 / WSCALE).then_inc(gelu_done, 1)

            def experts(b):
                for x in range(HT):
                    if x % 4 == 3:
                        p = x // 4
                        act.wait_ge(spread_done, b * PAIRS + p + 1)
                        if not (isinstance(b, int) and p < 2):
                            act.wait_ge(term_ready, b * PAIRS + p - 1)
                        nc.scalar.activation(wspread[:, p % 2, :], banks(6, 2), ACT.Copy).then_inc(spread_copied, 1)
                    if not (isinstance(b, int) and x < 2):
                        gelu(b, x)

            gelu(0, 0)
            gelu(0, 1)
            act.wait_ge(wT_cleared, 1)
            for c in range(B + 1):
                act.wait_ge(wT_done, c + 1)
                nc.scalar.activation(wT[0:64, wT_cols(c)], banks(*w_banks(c))[0:64, 0:wT_count(c)], ACT.Copy).then_inc(wT_hi, 1)
            act.wait_ge(hcls_biased, 1)
            nc.scalar.activation(hcls[:, :, :], hcls[:, :, :], ACT.Gelu).then_inc(hcls_gelu, 1)
            experts(0)
            with act.Fori(1, B) as b:
                experts(b)
            act.wait_ge(ocls_step, 4)
            act.dma_start(out[:, 0, :], h_tok[0:B, B * TILES, :]).then_inc(stored, 16)

        @block.vector
        def _(dve):
            nc.vector.memset(h_tok[:, B * TILES, :], 0.0).then_inc(clstok_cleared, 1)
            nc.vector.memset(b2f[:, :], 0.0).then_inc(b2_cleared, 1)
            dve.wait_ge(ident_landed, 16)
            nc.vector.tensor_copy(ident16[:, :], ident32[:, :]).then_inc(ident16_set, 1)
            nc.vector.tensor_tensor(fold[:, :], ident32[:, 0:D], ident32[:, D:2 * D], ALU.add).then_inc(ident16_set, 1)
            nc.vector.memset(xT[D:D + 1, :], 1.0).then_inc(ones_set, 1)
            nc.vector.memset(QA[64:96, :], 0.0).then_inc(ones_set, 1)
            nc.vector.memset(Vt[:, :, D:D + 1], 1.0).then_inc(ones_set, 1)
            dve.wait_ge(emb_w_summed, 1)
            for k in range(-(-OGROUPS // OBANK)):
                o = OG * OBANK * k
                m = min(OG * OBANK, 64 - o)
                for h in range(2):
                    rows = slice(64 * h, 64 * h + 64)
                    nc.vector.tensor_copy(G[rows, :, :, o:o + m], ps[rows, k, 0:PATCH * m].rearrange(
                        "p (o h a q) -> p h q a o", h=2, a=2, q=4)[:, h]).then_inc(emb_w_ready, 1)
            dve.wait_ge(aug_landed, 48)
            nc.vector.tensor_scalar(qtab_sb[96:128, :], qtab_sb[96:128, :], qcol[96:128, 0:1], None, ALU.mult).then_inc(qaug_scaled, 1)
            dve.wait_ge(qaug_scaled, 1)
            nc.vector.tensor_copy(qhi[96:128, :], qtab_sb[96:128, :]).then_inc(qaug_split, 1)
            dve.wait_ge(qaug_split, 1)
            nc.vector.scalar_tensor_tensor(QA[96:128, 0:SEQ], qhi[96:128, 0:SEQ], qcol[96:128, 1:2],
                                           qtab_sb[96:128, 0:SEQ], ALU.mult, ALU.add).then_inc(qaug_ready, 1)
            nc.vector.scalar_tensor_tensor(QA[96:128, CLS:COLS], qhi[96:128, SEQ:SEQ + B], qcol[96:128, 1:2],
                                           qtab_sb[96:128, SEQ:SEQ + B], ALU.mult, ALU.add).then_inc(qaug_ready, 1)
            dve.wait_ge(qaug_ready, 1)
            for b in range(1, B):
                nc.vector.tensor_copy(QA[96:128, b * SEQ:(b + 1) * SEQ], QA[96:128, 0:SEQ]).then_inc(qaug_ready, 1)

            def spread(a, shape):
                return a.unsqueeze(2).broadcast_to(shape)

            def norm_centre(k, src, rows, tiles):
                r, s = slice(0, rows), slice(0, tiles)
                nc.vector.tensor_reduce(stats[r, 0, s], src, AX_X, ALU.add).then_inc(ln_sum, 1)
                dve.wait_ge(ln_sum, k + 1)
                nc.vector.tensor_scalar(stats[r, 1, s], stats[r, 0, s], 1.0 / D, None, ALU.mult).then_inc(ln_mean, 1)
                dve.wait_ge(ln_mean, k + 1)
                nc.vector.tensor_tensor(centred[r, s, :], src, spread(stats[r, 1, s], [rows, tiles, D]), ALU.subtract).then_inc(ln_centred, 1)

            def norm_variance(k, rows, tiles):
                r, s = slice(0, rows), slice(0, tiles)
                dve.wait_ge(ln_squared, k + 1)
                nc.vector.tensor_reduce(stats[r, 2, s], squares[r, s, :], AX_X, ALU.add).then_inc(ln_sumsq, 1)
                dve.wait_ge(ln_sumsq, k + 1)
                nc.vector.tensor_scalar(stats[r, 3, s], stats[r, 2, s], 1.0 / D, EPS, ALU.mult, ALU.add).then_inc(ln_var, 1)

            def norm_scale(k, rows, tiles):
                r, s = slice(0, rows), slice(0, tiles)
                dve.wait_ge(ln_rstd, k + 1)
                nc.vector.tensor_tensor(normed[r, s, 0, :], centred[r, s, :], spread(stats[r, 4, s], [rows, tiles, D]), ALU.mult).then_inc(ln_done, 1)

            def take_transposed(k, n):
                dve.wait_ge(norm_T, k + 1)
                nc.vector.tensor_copy(xT[0:D, 0:n], banks(4, 2)[0:D, 0:n]).then_inc(xT_copied, 1)

            def project_lo(k, cols, n):
                dve.wait_ge(q_hi, k + 1)
                nc.vector.tensor_copy(QA[0:64, cols], QB[0:64, cols]).then_inc(hi_again, 1)
                nc.vector.scalar_tensor_tensor(QB[64:128, cols], banks(6, 2)[0:64, 0:n], QSCALE, QB[0:64, cols],
                                               ALU.mult, ALU.subtract).then_inc(q_lo, 1)
                dve.wait_ge(k_hi, k + 1)
                nc.vector.tensor_copy(KA[0:64, cols], KB[64:128, cols]).then_inc(hi_again, 1)
                nc.vector.tensor_tensor(KB[0:64, cols], banks(6, 2)[64:128, 0:n], KB[64:128, cols], ALU.subtract).then_inc(k_lo, 1)

            def take_values(k, tiles, n, rows):
                dve.wait_ge(v_done, k + 1)
                nc.vector.tensor_copy(Vt[0:rows, tiles, 0:D], ps[0:rows, 4, 0:D * (n // rows)].rearrange("p (t d) -> p t d", d=D)).then_inc(v_copied, 1)

            def take_tokens(b):
                dve.wait_ge(tok_done, b + 1)
                tokens = h_tok[:, bass.ds(b * TILES, TILES), :]
                nc.vector.tensor_copy(tokens, ps[:, 3, :].rearrange("p (t d) -> p t d", d=D)).then_inc(tok_copied, 1)
                apart(dve)
                dve.wait_ge(tok_copied, b + 1)
                norm_centre(b, tokens, 128, TILES)

            take_tokens(0)
            norm_variance(0, 128, TILES)
            norm_scale(0, 128, TILES)
            with dve.Fori(0, B - 1) as b:
                take_tokens(b + 1)
                take_transposed(b, SEQ)
                norm_variance(b + 1, 128, TILES)
                norm_scale(b + 1, 128, TILES)
                project_lo(b, bass.ds(b * SEQ, SEQ), SEQ)
                take_values(b, bass.ds(b * TILES, TILES), SEQ, 128)
            dve.wait_ge(cls_landed, 16)
            norm_centre(B, h_tok[0:B, B * TILES:B * TILES + 1, :], B, 1)
            take_transposed(B - 1, SEQ)
            norm_variance(B, B, 1)
            norm_scale(B, B, 1)
            project_lo(B - 1, slice((B - 1) * SEQ, B * SEQ), SEQ)
            take_values(B - 1, slice((B - 1) * TILES, B * TILES), SEQ, 128)
            take_transposed(B, B)
            project_lo(B, slice(CLS, COLS), B)
            take_values(B, slice(B * TILES, B * TILES + 1), B, B)
            dve.wait_ge(w1_hi, 2)
            nc.vector.scalar_tensor_tensor(WB[:, :], w1f[:, 0:E * H], WSCALE, WA[:, :], ALU.mult, ALU.subtract).then_inc(w1_lo, 1)
            nc.vector.scalar_tensor_tensor(GB[:, :], wgf[:, :], WSCALE, GA[:, :], ALU.mult, ALU.subtract).then_inc(w1_lo, 1)
            dve.wait_ge(b2_hi, 1)
            nc.vector.tensor_tensor(B2B[:, :], b2f[:, :], B2A[:, :], ALU.subtract).then_inc(b2_lo, 1)

            def maxima(b):
                if not isinstance(b, int):
                    dve.wait_ge(mcls_ready, b)
                dve.wait_ge(side_full[0], side(b, 0, 0))
                nc.vector.tensor_copy(mpart[:, :, 2], ps[:, 6, 0:TILES]).then_inc(mcls_max, 1)
                nc.vector.tensor_copy(mcls[:, 2:3], ps[0:1, 6, TILES:TILES + 1]).then_inc(side_free[0], 1)
                for k in range(2):
                    dve.wait_ge(side_full[k], side(b, 1, k))
                    nc.vector.tensor_reduce(mcls[:, k:k + 1], ps[0:1, 6 + k, :], AX_X, ALU.max).then_inc(side_free[k], 1)
                for i in range(TILES):
                    for k in range(2):
                        dve.wait_ge(side_full[k], side(b, 2 + i, k))
                        nc.vector.tensor_reduce(mpart[:, i, k:k + 1], ps[:, 6 + k, :], AX_X, ALU.max).then_inc(side_free[k], 1)
                for k in range(2):
                    dve.wait_ge(side_free[k], side(b, 9, k))
                nc.vector.tensor_reduce(mneg[:, :], mpart[:, :, :], AX_X, ALU.max, negate=True).then_inc(m_ready, 1)
                nc.vector.tensor_reduce(QA[64:65, bass.ds(CLS + b, 1)], mcls[:, 0:3], AX_X, ALU.max, negate=True).then_inc(mcls_ready, 1)

            def normalise(b):
                sums = ps[:, 4:6, 0:4 * (D + 1)].rearrange("p a (i d) -> p a i d", d=D + 1)
                dve.wait_ge(acc_done, b + 2)
                nc.vector.reciprocal(rden[:, :].rearrange("p (a i) -> p a i", a=2), sums[:, :, :, D]).then_inc(acc_recip, 1)
                dve.wait_ge(acc_recip, b + 1)
                dve.wait_ge(attn_added, b + 1)
                r = rden[:, :].rearrange("p (a i) -> p a i", a=2).unsqueeze(3).broadcast_to([128, 2, 4, D])
                nc.vector.tensor_tensor(attn[:, :, :].rearrange("p (a i) d -> p a i d", a=2), sums[:, :, :, 0:D], r, ALU.mult).then_inc(acc_free, 1)

            dve.sem_inc(acc_free, 1)
            maxima(0)
            with dve.Fori(0, B - 1) as b:
                maxima(b + 1)
                normalise(b)
            normalise(B - 1)
            dve.wait_ge(cq_acc, 1)
            dve.wait_ge(acc_free, B + 1)
            nc.vector.reciprocal(rden[0:B, 0:1], ps[0:B, 7, D:D + 1]).then_inc(acc_recip, 1)
            dve.wait_ge(acc_recip, B + 1)
            dve.wait_ge(attn_added, B + 1)
            nc.vector.tensor_scalar(attn[0:B, 0, :], ps[0:B, 7, 0:D], rden[0:B, 0:1], None, ALU.mult).then_inc(acc_free, 1)

            nc.vector.memset(wcur, 0.0).then_inc(wcur_cleared, 1)
            dve.wait_ge(w1_lo, 1)
            nc.vector.memset(wT[64:128, :], 0.0).then_inc(wT_cleared, 1)
            dve.wait_ge(attn_added, B + 2)
            for c in range(B + 1):
                k, s = B + 1 + c, tiles_of(c)
                nc.vector.tensor_reduce(stats2[:, 0, s], h_tok[:, s, :], AX_X, ALU.add).then_inc(ln_sum, 1)
                dve.wait_ge(ln_sum, k + 1)
                nc.vector.tensor_scalar(stats2[:, 1, s], stats2[:, 0, s], 1.0 / D, None, ALU.mult).then_inc(ln_mean, 1)
                dve.wait_ge(ln_mean, k + 1)
                nc.vector.tensor_tensor(centred2[:, s, :], h_tok[:, s, :], spread(stats2[:, 1, s], [128, tile_count(c), D]),
                                        ALU.subtract).then_inc(ln_centred, 1)
            for c in range(B + 1):
                k, s = B + 1 + c, tiles_of(c)
                dve.wait_ge(ln_squared, k + 1)
                nc.vector.tensor_reduce(stats2[:, 2, s], squares2[:, s, :], AX_X, ALU.add).then_inc(ln_sumsq, 1)
                dve.wait_ge(ln_sumsq, k + 1)
                nc.vector.tensor_scalar(stats2[:, 3, s], stats2[:, 2, s], 1.0 / D, EPS, ALU.mult, ALU.add).then_inc(ln_var, 1)
            for c in range(B + 1):
                k, s = B + 1 + c, tiles_of(c)
                dve.wait_ge(ln_rstd, k + 1)
                nc.vector.tensor_tensor(normed2[:, s, :], centred2[:, s, :], spread(stats2[:, 4, s], [128, tile_count(c), D]),
                                        ALU.mult).then_inc(ln_done, 1)
            for c in range(B + 1):
                dve.wait_ge(f_hi, c + 1)
                nc.vector.tensor_tensor(FA[64:128, tokens_of(c)], banks(*norm_banks(c))[0:64, 0:128 * tile_count(c)],
                                        FA[0:64, tokens_of(c)], ALU.subtract).then_inc(f_lo, 1)

            steps = [0]

            def done(ins):
                steps[0] += 1
                ins.then_inc(gate_step, 1)
                dve.wait_ge(gate_step, steps[0])

            dve.wait_ge(gate_done, 1)
            done(nc.vector.scalar_tensor_tensor(logits[:, :, :], ps[:, 4, 0:E * ALL].rearrange("p (t e) -> p t e", e=E), 1.0 / WSCALE,
                                                bg_sb[:, :].unsqueeze(1).broadcast_to([128, ALL, E]), ALU.mult, ALU.add))
            done(nc.vector.tensor_reduce(top[:, :], logits[:, :, :], AX_X, ALU.max))
            done(nc.vector.tensor_tensor(chosen[:, :, :], logits[:, :, :], top[:, :].unsqueeze(2).broadcast_to([128, ALL, E]), ALU.subtract))
            done(nc.vector.tensor_tensor(diff, logits[:, :, :].unsqueeze(2).broadcast_to([128, ALL, E, E]),
                                         logits[:, :, :].unsqueeze(3).broadcast_to([128, ALL, E, E]), ALU.subtract))
            flat = lambda t: t.rearrange("p t e f -> p t (e f)")
            done(nc.vector.scalar_tensor_tensor(flat(equal), flat(diff), 0.0, before_sb[:, :].unsqueeze(1).broadcast_to([128, ALL, E * E]),
                                                ALU.is_equal, ALU.mult))
            done(nc.vector.scalar_tensor_tensor(flat(diff), flat(diff), 0.0, flat(equal), ALU.is_gt, ALU.add))
            done(nc.vector.tensor_reduce(rank[:, :, :], diff, AX_X, ALU.add))
            dve.wait_ge(gate_exp, 1)
            done(nc.vector.scalar_tensor_tensor(chosen[:, :, :], rank[:, :, :], 2.0, expd[:, :, :], ALU.is_lt, ALU.mult))
            done(nc.vector.tensor_reduce(csum[:, 0, :], chosen[:, :, :], AX_X, ALU.add))
            done(nc.vector.reciprocal(csum[:, 1, :], csum[:, 0, :]))
            dve.wait_ge(wcur_cleared, 1)
            for g in range(2):
                nc.vector.tensor_tensor(wcur[:, :, g, 0:E], chosen[:, :, :], csum[:, 1, :].unsqueeze(2).broadcast_to([128, ALL, E]),
                                        ALU.mult).then_inc(w_ready, 1)
            for c in range(B + 1):
                dve.wait_ge(wT_hi, c + 1)
                nc.vector.tensor_tensor(wT[32:32 + E, wT_cols(c)], banks(*w_banks(c))[32:32 + E, 0:wT_count(c)],
                                        wT[32:32 + E, wT_cols(c)], ALU.subtract).then_inc(wT_lo, 1)

            mine = h_tok[0:B, B * TILES, :]
            dve.wait_ge(hcls_done, 1)
            nc.vector.scalar_tensor_tensor(hcls[:, :, :], ps[:, 6, 0:HT * B].rearrange("p (n c) -> p n c", c=B), 1.0 / WSCALE,
                                           b1_sb[:, :].unsqueeze(2).broadcast_to([128, HT, B]), ALU.mult, ALU.add).then_inc(hcls_biased, 1)
            dve.wait_ge(ocls_done, 1)
            dve.wait_ge(w_ready, 2)
            nc.vector.tensor_tensor(ocls[:, :, :], ps[0:B, 7, :].rearrange("p (e d) -> p e d", d=D),
                                    wcur[0:B, B * TILES, 0, 0:E].unsqueeze(2).broadcast_to([B, E, D]), ALU.mult).then_inc(ocls_step, 1)
            nc.vector.tensor_tensor(mine, ps[0:B, 6, HT * B:HT * B + D], mine, ALU.add).then_inc(ocls_step, 1)
            dve.wait_ge(ocls_step, 2)
            nc.vector.tensor_reduce(scls[:, :], ocls[:, :, :].rearrange("p e d -> p d e"), AX_X, ALU.add).then_inc(ocls_step, 1)
            dve.wait_ge(ocls_step, 3)
            nc.vector.tensor_tensor(mine, mine, scls[:, :], ALU.add).then_inc(ocls_step, 1)

            def add_tokens(b):
                tokens = h_tok[:, bass.ds(b * TILES, TILES), :]
                apart(dve)
                dve.wait_ge(fold_done, b + 1)
                nc.vector.tensor_tensor(tokens, ps[:, 6, :].rearrange("p (t d) -> p t d", d=D), tokens, ALU.add).then_inc(tokens_done, 1)

            def experts(b):
                for p in range(PAIRS):
                    if p == 0 and not isinstance(b, int):
                        add_tokens(b - 1)
                    dve.wait_ge(spread_copied, b * PAIRS + p + 1)
                    dve.wait_ge(pair_done, b * PAIRS + p + 1)
                    if p == 0:
                        nc.vector.tensor_tensor(esum, banks(4, 2), wspread[:, 0, :], ALU.mult).then_inc(term_ready, 1)
                    else:
                        if not (isinstance(b, int) and p == 1):
                            dve.wait_ge(sum_ready, b * (PAIRS - 1) + p - 1)
                        nc.vector.tensor_tensor(eterm, banks(4, 2), wspread[:, p % 2, :], ALU.mult).then_inc(term_ready, 1)
                        dve.wait_ge(term_ready, b * PAIRS + p + 1)
                        nc.vector.tensor_tensor(esum, esum, eterm, ALU.add).then_inc(sum_ready, 1)

            experts(0)
            with dve.Fori(1, B) as b:
                experts(b)
            add_tokens(B - 1)

        @block.gpsimd
        def _(pool):
            nc.gpsimd.memset(half[:, :], -0.5).then_inc(consts_set, 1)
            nc.gpsimd.memset(Pz[:, :], 0.0).then_inc(consts_set, 1)
            nc.gpsimd.memset(normed[:, :, 1, :], 0.0).then_inc(ones_set, 1)
            nc.gpsimd.memset(FA[:, CLS + 128:CLS + SEQ], 0.0).then_inc(ones_set, 1)

            def rstd(k, rows, tiles):
                pool.wait_ge(ln_var, k + 1)
                r, s = slice(0, rows), slice(0, tiles)
                nc.gpsimd.tensor_tensor(stats[r, 4, s], stats[r, 3, s], half[r, s], ALU.pow).then_inc(ln_rstd, 1)

            pool.wait_ge(consts_set, 2)
            with pool.Fori(0, B) as b:
                rstd(b, 128, TILES)
            rstd(B, B, 1)

            pool.sem_inc(attn_added, 1)
            with pool.Fori(0, B) as b:
                apart(pool)
                pool.wait_ge(acc_free, b + 2)
                tokens = h_tok[:, bass.ds(b * TILES, TILES), :]
                nc.gpsimd.tensor_tensor(tokens, tokens, attn[:, :, :], ALU.add).then_inc(attn_added, 1)
            pool.wait_ge(acc_free, B + 2)
            tokens = h_tok[0:B, B * TILES, :]
            nc.gpsimd.tensor_tensor(tokens, tokens, attn[0:B, 0, :], ALU.add).then_inc(attn_added, 1)

            for c in range(B + 1):
                pool.wait_ge(ln_var, B + 1 + c + 1)
                nc.gpsimd.tensor_tensor(stats2[:, 4, tiles_of(c)], stats2[:, 3, tiles_of(c)], half[:, 0:tile_count(c)], ALU.pow).then_inc(ln_rstd, 1)

        @block.tensor
        def _(pe):
            pe.wait_ge(emb_w_landed, 32)
            for r in range(OGROUPS):
                at = OG * PATCH * (r % OBANK)
                last = nc.tensor.matmul(ps[:, r // OBANK, at:at + OG * PATCH], wf_sb[:, r, :], dft_sb[:, :], start=True, stop=True)
            last.then_inc(emb_w_summed, 1)

            def embed(b, first):
                pe.wait_ge(x_ready, b + 1)
                if not first:
                    pe.wait_ge(parts_copied, 2 * b)
                blocks = xs[:, bass.ds(b * XB, XB)].rearrange("p (j q v) -> p j q v", q=4, v=V)
                for c, j0 in enumerate(range(0, NBLK, 8)):
                    j1 = min(j0 + 8, NBLK)
                    for q in range(4):
                        last = nc.tensor.matmul(ps[:, c, 0:V * (j1 - j0)], G[:, q, :, :].rearrange("p a o -> p (a o)"),
                                                blocks[:, j0:j1, q, :], start=(q == 0), stop=(q == 3))
                last.then_inc(emb_done, 1)

            def sum_halves(b, first):
                pe.wait_ge(parts_copied, 2 * (b + 1))
                if not first:
                    pe.wait_ge(tok_copied, b)
                for i in range(TILES):
                    last = nc.tensor.matmul(ps[:, 3, D * i:D * i + D], parts[:, 128 * i:128 * i + 128], fold[:, :], start=True, stop=True)
                last.then_inc(tok_done, 1)

            def projections(k, tiles, rows, first):
                pe.wait_ge(ln_done, k + 1)
                if not first:
                    pe.wait_ge(v_copied, k)
                for i in range(tiles):
                    last = nc.tensor.transpose(banks(4, 2)[:, 128 * i:128 * i + rows], normed[0:rows, i, :, :].rearrange("p g d -> p (g d)"), ident32[0:rows, 0:rows])
                last.then_inc(norm_T, 1)
                n = rows * tiles
                pe.wait_ge(xT_copied, k + 1)
                if not first:
                    pe.wait_ge(q_lo, k)
                    pe.wait_ge(k_lo, k)
                for c in range(0, n, 512):
                    m = min(512, n - c)
                    last = nc.tensor.matmul(ps[:, 6 + c // 512, 0:m], wqk_sb[:, :], xT[:, c:c + m], start=True, stop=True)
                last.then_inc(qk_done, 1)
                for i in range(tiles):
                    last = nc.tensor.matmul(ps[0:rows, 4, D * i:D * i + D], xT[:, i * 128:i * 128 + rows], wv_sb[:, :], start=True, stop=True)
                last.then_inc(v_done, 1)

            pe.wait_ge(emb_w_ready, 6)
            embed(0, True)
            pe.wait_ge(ident_landed, 16)
            pe.wait_ge(ident16_set, 2)
            sum_halves(0, True)
            pe.wait_ge(proj_w_landed, 32)
            pe.wait_ge(ones_set, 5)
            embed(1, False)
            sum_halves(1, False)
            projections(0, TILES, 128, True)
            embed(2, False)
            with pe.Fori(1, B - 2) as b:
                sum_halves(b + 1, False)
                projections(b, TILES, 128, False)
                embed(b + 2, False)
            sum_halves(B - 1, False)
            projections(B - 2, TILES, 128, False)
            projections(B - 1, TILES, 128, False)
            projections(B, 1, B, False)

            def cols(b, t, n):
                return bass.ds(b * SEQ + t, n)

            def own(b, turn, bank):
                before_it = side(b, turn, bank) - 1
                if not (isinstance(before_it, int) and before_it == 0):
                    pe.wait_ge(side_free[bank], before_it)

            def turn(b, n):
                if n == 0:
                    own(b, n, 0)
                    for i in range(TILES):
                        nc.tensor.matmul(ps[:, 6, i:i + 1], QA[:, cols(b, 128 * i, 128)], KA[:, CLS:CLS + 1], start=True, stop=True)
                    nc.tensor.matmul(ps[0:1, 6, TILES:TILES + 1], QA[:, COLS - 1:COLS], KA[:, CLS:CLS + 1],
                                     start=True, stop=True).then_inc(side_full[0], 1)
                elif n == 1:
                    for k in range(2):
                        own(b, n, k)
                        nc.tensor.matmul(ps[0:1, 6 + k, :], QA[:, COLS - 1:COLS], KA[:, cols(b, 512 * k, 512)],
                                         start=True, stop=True).then_inc(side_full[k], 1)
                elif n < 10:
                    for k in range(2):
                        own(b, n, k)
                        nc.tensor.matmul(ps[:, 6 + k, :], QA[:, cols(b, 128 * (n - 2), 128)], KA[:, cols(b, 512 * k, 512)],
                                         start=True, stop=True).then_inc(side_full[k], 1)
                elif n == 10:
                    pe.wait_ge(m_ready, b + 1)
                    for k in range(2):
                        own(b, n, k)
                        for i in range(4):
                            last = nc.tensor.matmul(ps[64:65, 6 + k, 128 * i:128 * i + 128], mneg[:, 4 * k + i:4 * k + i + 1],
                                                    ident16[:, :], start=True, stop=True)
                        last.then_inc(side_full[k], 1)
                else:
                    for k in range(2):
                        own(b, n, k)
                    for k in range(2):
                        for g, (KX, QX) in enumerate(((KA, QA), (KB, QB))):
                            last = nc.tensor.matmul(ps[0:1, 6 + k, :], KX[:, CLS:CLS + 1], QX[:, cols(b, 512 * k, 512)],
                                                    start=(g == 0), stop=(g == 1))
                        last.then_inc(side_full[k], 1)

            def scores(b, t):
                pe.wait_ge(exp_done, b * TILES + t + 1)
                pair = 2 * (t % 2)
                for g, (KX, QX) in enumerate(((KA, QA), (KB, QB))):
                    for k in range(2):
                        last = nc.tensor.matmul(ps[:, pair + k, :], KX[:, cols(b, 128 * t, 128)], QX[:, cols(b, 512 * k, 512)],
                                                start=(g == 0), stop=(g == 1))
                last.then_inc(score_done, 1)

            def sum_tile(i):
                return ps[:, 4 + i // 4, (D + 1) * (i % 4):(D + 1) * (i % 4 + 1)]

            def values(b, t):
                pe.wait_ge(exp_done, b * TILES + t + 1 + SCORE_RING)
                if t == 0:
                    pe.wait_ge(acc_free, b + 1)
                for i in range(TILES):
                    last = nc.tensor.matmul(sum_tile(i), P[:, t % P_RING, 128 * i:128 * i + 128], Vt[:, bass.ds(b * TILES + t, 1), :],
                                            start=(t == 0 and i % 4 == 0), stop=False, skip_group_check=True)
                last.then_inc(pv_done, 1)

            def class_values(b):
                for k in range(2):
                    pe.wait_ge(side_free[k], side(b, 11, k))
                for i in range(TILES):
                    last = nc.tensor.matmul(sum_tile(i), Pc[:, 128 * i:128 * i + 128], Vt[0:1, B * TILES, :],
                                            start=False, stop=True, skip_group_check=True)
                last.then_inc(acc_done, 1)

            def attend(b, more):
                turn(b, 11)
                scores(b, 0)
                scores(b, 1)
                for t in range(TILES):
                    values(b, t)
                    if t + 2 < TILES:
                        scores(b, t + 2)
                    if more:
                        for n in TURNS[t]:
                            turn(b + 1, n)
                class_values(b)

            TURNS = [[0, 1], [2, 3], [4, 5], [6, 7], [8, 9], [], [10], []]
            pe.sem_inc(pv_done, P_RING)
            pe.sem_inc(acc_done, 1)
            pe.wait_ge(q_lo, B + 1)
            pe.wait_ge(k_lo, B + 1)
            pe.wait_ge(hi_again, 2 * (B + 1))
            pe.wait_ge(v_copied, B + 1)
            pe.wait_ge(qaug_ready, B + 1)
            pe.wait_ge(ktab_landed, 16 * (B + 1))
            for n in range(11):
                turn(0, n)
            with pe.Fori(0, B - 1) as b:
                attend(b, True)
            attend(B - 1, False)

            pe.wait_ge(mcls_ready, B)
            pe.wait_ge(side_free[0], B * USES[0])
            with pe.Fori(0, B) as b:
                for t in range(TILES):
                    for g, (KX, QX) in enumerate(((KA, QA), (KB, QB))):
                        nc.tensor.matmul(ps[:, 6, bass.ds(b * TILES + t, 1)], KX[:, cols(b, 128 * t, 128)], QX[:, bass.ds(CLS + b, 1)],
                                         start=(g == 0), stop=(g == 1))
            for g, (KX, QX) in enumerate(((KA, QA), (KB, QB))):
                last = nc.tensor.matmul(ps[0:1, 6, B * TILES:B * TILES + B], KX[:, CLS:CLS + 1], QX[:, CLS:COLS], start=(g == 0), stop=(g == 1))
            last.then_inc(cq_scored, 1)
            pe.wait_ge(cq_exp, 2)
            pe.wait_ge(side_free[1], B * USES[1])
            for u in range(B * TILES):
                bb, t = divmod(u, TILES)
                nc.tensor.matmul(ps[0:B, 7, 0:D + 1], Pz[:, 33 * bb + 4 * t - bb:33 * bb + 4 * t - bb + B], Vt[:, u, :],
                                 start=(u == 0), stop=False)
            nc.tensor.matmul(ps[0:B, 7, 0:D + 1], Pzc[:, :], Vt[0:1, B * TILES, :], start=False, stop=True).then_inc(cq_acc, 1)

            pe.wait_ge(acc_free, B + 1)
            for c in range(B + 1):
                pe.wait_ge(ln_done, B + 1 + c + 1)
                if c >= 2:
                    pe.wait_ge(f_lo, c - 1)
                for i in range(tile_count(c)):
                    last = nc.tensor.transpose(banks(*norm_banks(c))[0:D, 128 * i:128 * i + 128], normed2[:, c * TILES + i, :], ident32[:, :])
                last.then_inc(n2_T, 1)
            pe.wait_ge(w1_lo, 2)
            for c in range(B + 1):
                pe.wait_ge(f_lo, c + 1)
                for i in range(c * TILES, c * TILES + tile_count(c)):
                    for g, W in enumerate((GA, GB)):
                        last = nc.tensor.matmul(ps[:, 4, E * i:E * i + E], FA[:, 128 * i:128 * i + 128], W[:, :], start=(g == 0), stop=(g == 1))
            last.then_inc(gate_done, 1)

            def hidden(b, x):
                n = tile_at(x)
                if not (isinstance(b, int) and b == 0 and x < 2):
                    pe.wait_ge(gelu_done, b * HT + x - 1)
                for g, W in enumerate((WA, WB)):
                    for k in range(2):
                        last = nc.tensor.matmul(ps[:, 2 * (x % 2) + k, :], W[:, 128 * n:128 * n + 128], FA[:, cols(b, 512 * k, 512)],
                                                start=(g == 0), stop=(g == 1))
                last.then_inc(hid_done, 1)

            def outputs(b, u):
                pe.wait_ge(gelu_done, b * HT + 2 * u + 2)
                if u % 2 == 0 and not (isinstance(b, int) and u == 0):
                    pe.wait_ge(term_ready, b * PAIRS + u // 2)
                for k in range(2):
                    for o in range(2):
                        x = 2 * u + o
                        last = nc.tensor.matmul(ps[64 * o:64 * o + 64, 4 + k, :], w2_sb[:, tile_at(x), :], hid[:, x % 4, 512 * k:512 * k + 512],
                                                start=(u % 2 == 0), stop=(u % 2 == 1))
                if u % 2 == 1:
                    last.then_inc(pair_done, 1)
                    pe.wait_ge(pair_done, b * PAIRS + u // 2 + 1)
                    pe.sem_inc(step_used, 1)
                else:
                    last.then_inc(step_used, 1)

            def spread_weights(b, p):
                if not (isinstance(b, int) and p == 0):
                    pe.wait_ge(spread_copied, b * PAIRS + p)
                if p == 1 and not isinstance(b, int):
                    pe.wait_ge(tokens_done, b)
                for k in range(2):
                    last = nc.tensor.matmul(ps[:, 6 + k, :], sel_sb[:, p, :], wT[:, cols(b, 512 * k, 512)], start=True, stop=True)
                last.then_inc(spread_done, 1)

            def fold_sum(b):
                pe.wait_ge(sum_ready, (b + 1) * (PAIRS - 1))
                for i in range(TILES):
                    to = ps[:, 6, D * i:D * i + D]
                    nc.tensor.matmul(to, esum[:, 128 * i:128 * i + 128], fold[:, :], start=True, stop=False)
                    nc.tensor.matmul(to, wT[:, cols(b, 128 * i, 128)], B2A[:, :], start=False, stop=False)
                    last = nc.tensor.matmul(to, wT[:, cols(b, 128 * i, 128)], B2B[:, :], start=False, stop=True)
                last.then_inc(fold_done, 1)

            def experts(b):
                for u in range(HT // 2):
                    for x in (2 * u + 2, 2 * u + 3):
                        if x < HT:
                            hidden(b, x)
                        else:
                            hidden(b + 1, x - HT)
                    if u % 2 == 0:
                        spread_weights(b, u // 2)
                    outputs(b, u)
                    if u == 0 and not isinstance(b, int):
                        pe.wait_ge(spread_copied, b * PAIRS + 1)
                        fold_sum(b - 1)

            hidden(0, 0)
            hidden(0, 1)
            pe.wait_ge(w_ready, 2)
            for c in range(B + 1):
                if c >= 2:
                    pe.wait_ge(wT_lo, c - 1)
                for i in range(tile_count(c)):
                    last = nc.tensor.transpose(banks(*w_banks(c))[0:64, 128 * i:128 * i + 128],
                                               wcur[:, c * TILES + i, :, :].rearrange("p g e -> p (g e)"), ident32[:, :])
                last.then_inc(wT_done, 1)
            pe.wait_ge(wT_lo, B + 1)
            for n in range(HT):
                for g, W in enumerate((WA, WB)):
                    nc.tensor.matmul(ps[:, 6, B * n:B * n + B], W[:, 128 * n:128 * n + 128], FA[:, CLS:COLS], start=(g == 0), stop=(g == 1))
            pe.wait_ge(b2_lo, 1)
            for g, W in enumerate((B2A, B2B)):
                last = nc.tensor.matmul(ps[0:B, 6, B * HT:B * HT + D], wT[:, CLS:COLS], W[:, :], start=(g == 0), stop=(g == 1))
            last.then_inc(hcls_done, 1)
            pe.wait_ge(hcls_gelu, 1)
            for e in range(E):
                for j in range(2):
                    last = nc.tensor.matmul(ps[0:B, 7, D * e:D * e + D], hcls[:, 2 * e + j, :], w2_sb[:, 2 * e + j, :], start=(j == 0), stop=(j == 1))
            last.then_inc(ocls_done, 1)
            pe.wait_ge(ocls_step, 2)
            pe.wait_ge(ffn_w_landed, 80)
            experts(0)
            with pe.Fori(1, B) as b:
                experts(b)
            pe.wait_ge(spread_copied, B * PAIRS)
            fold_sum(B - 1)


def _tables():
    f, p = np.arange(PATCH // 2 + 1)[:, None], np.arange(PATCH)[None, :]
    angle = 2 * np.pi * f * p / PATCH
    by_step = np.concatenate([np.cos(angle), -np.sin(angle)]) / np.sqrt(PATCH)
    one = by_step.reshape(NF, 2, 2, 4).transpose(0, 2, 1, 3).reshape(NF, PATCH)
    dft = np.kron(np.eye(OG), one)
    pos = np.concatenate([np.arange(1, SEQ + 1), np.zeros(B)])
    trig = np.stack([g(2 * np.pi * pos / period) for period in PERIODS for g in (np.cos, np.sin)])
    hi = trig.astype(np.float16)
    lo = (trig - hi).astype(np.float16)
    qtab = np.zeros((32, SEQ + B), np.float32)
    qtab[0:12] = np.tile(trig, (3, 1))
    negmask = np.zeros((32, 1), np.float32)
    negmask[8:12] = -1
    ktab = np.zeros((64, SEQ + B), np.float16)
    ktab[0] = 1
    ktab[32:44] = np.concatenate([hi, lo, hi])
    before = (np.arange(E)[None, :] < np.arange(E)[:, None]).astype(np.float32).reshape(1, E * E)
    sel = np.zeros((128, E // 2, 128), np.float16)
    for e in range(E):
        for g in range(2):
            sel[32 * g + e, e // 2, 64 * (e % 2):64 * (e % 2) + 64] = 1
    return {"sel": sel.reshape(128, -1), "dft": dft.astype(np.float32), "ident": np.eye(128, dtype=np.float32), "qtab": qtab, "ktab": ktab,
            "negmask": negmask, "before": before}


def kernel(x, cls_tok, L0_tok_W, L0_attn_Wq, L0_attn_bq, L0_attn_Wk, L0_attn_bk, L0_attn_Wv, L0_attn_bv, L0_attn_beta,
           L0_ffn_Wg, L0_ffn_bg, L0_ffn_W1, L0_ffn_b1, L0_ffn_W2, L0_ffn_b2):
    import concourse.bacc as bacc
    from concourse.bass_utils import run_bass_kernel_spmd

    def with_bias(w, b):
        w, b = np.asarray(w), np.asarray(b)
        return np.concatenate([w.T, b[None, :]])

    w = np.asarray(L0_tok_W).reshape(64, NF, C)
    wf = np.zeros((OGROUPS * OG, NF, 2, C), w.dtype)
    wf[0:64] = w[:, :, None, :]
    beta = np.asarray(L0_attn_beta)
    zeros = np.zeros((20, 1), np.float32)
    arrays = {
        "x": x, "cls_tok": cls_tok,
        "wf": wf.reshape(OGROUPS, OG, NF, 2 * C).transpose(1, 2, 0, 3).reshape(OG * NF, OGROUPS * 2 * C),
        "wqk": np.concatenate([with_bias(L0_attn_Wq, L0_attn_bq), with_bias(L0_attn_Wk, L0_attn_bk)], axis=1),
        "wv": with_bias(L0_attn_Wv, L0_attn_bv),
        "beta": np.concatenate([beta[[0, 0, 1, 1] * 3][:, None], zeros]),
        "wg": L0_ffn_Wg, "bg": L0_ffn_bg, "w1": L0_ffn_W1,
        "b1": np.asarray(L0_ffn_b1).reshape(HT, 128).T,
        "w2": L0_ffn_W2, "b2": L0_ffn_b2,
    }
    arrays.update(_tables())
    arrays = {k: np.ascontiguousarray(v) for k, v in arrays.items()}
    nc = bacc.Bacc("TRN2", target_bir_lowering=False, num_devices=1)
    aps = {k: nc.dram_tensor(f"{k}_dram", v.shape, mybir.dt.from_np(v.dtype), kind="ExternalInput").ap() for k, v in arrays.items()}
    out = nc.dram_tensor("out_dram", (B, SEQ + 1, D), F32, kind="ExternalOutput").ap()
    build(nc, out=out, **aps)
    r = run_bass_kernel_spmd(nc, [{f"{k}_dram": v for k, v in arrays.items()}], core_ids=[0])
    return r.results[0]["out_dram"]
```

```python
from contextlib import ExitStack

import numpy as np

import concourse.bass as bass
from concourse import mybir

F32 = mybir.dt.float32
F16 = mybir.dt.float16
ALU = mybir.AluOpType
ACT = mybir.ActivationFunctionType
AX_X = mybir.AxisListType.X

B, C, T, V = 4, 64, 128, 64
PATCH, STRIDE = 16, 8
NP = T // STRIDE
NBLK = NP + 1
NF = 2 * (PATCH // 2 + 1)
D = 64
SEQ = V * NP
TILES = SEQ // 128
ALL = B * TILES + 1
CLS = B * SEQ
COLS = CLS + B
E, H = 8, 256
HT = E * H // 128
EPS = 1e-5
WSCALE = 64.0
QSCALE = D ** -0.5
GATE_STEPS = 12
PERIODS = (24.0, 720.0)
XB = NBLK * 4 * V
OG = 128 // NF
OGROUPS = -(-64 // OG)
OBANK = 512 // (OG * PATCH)


def build(nc, x, cls_tok, wf, wqk, wv, beta, wg, bg, w1, b1, w2, b2,
          dft, ident, qtab, ktab, negmask, before, sel, out):
    ctx = ExitStack()
    with ctx:
        def sb(name, shape, dt=F32):
            return ctx.enter_context(nc.sbuf_tensor(name, shape, dt))

        def sem(name):
            return ctx.enter_context(nc.semaphore(name))

        xs = sb("xs", [128, B * XB])
        def later(first, n):
            assert first + n <= B * XB
            return xs[:, first:first + n]

        AD, AE = ALL * D, ALL * E * E
        P32 = later(4 * SEQ, 2 * SEQ).rearrange("p (r n) -> p r n", r=2)
        Phi, Plo = (later(2 * SEQ * k, 2 * SEQ).bitcast(F16).rearrange("p (r n) -> p r n", r=4) for k in range(2))
        hid = later(0, 4 * SEQ).rearrange("p (r n) -> p r n", r=4)
        wspread = later(4 * SEQ, 2 * SEQ).rearrange("p (r n) -> p r n", r=2)
        own = 6 * SEQ
        normed2 = later(own, AD).rearrange("p (t d) -> p t d", d=D)
        diff = later(own + AD, AE).rearrange("p (t e f) -> p t e f", e=E, f=E)
        equal = later(own + AD + AE, AE).rearrange("p (t e f) -> p t e f", e=E, f=E)
        wcur = later(own + AD + 2 * AE, AD).rearrange("p (t g e) -> p t g e", g=2, e=32)
        esum = later(own + 2 * AD + 2 * AE, SEQ)
        eterm = later(own + 2 * AD + 2 * AE + SEQ, SEQ)
        ident32 = sb("ident32", [128, 128])
        ident16 = sb("ident16", [128, 128], F16)
        wf_sb = sb("wf_sb", [OG * NF, OGROUPS, 128])
        dft_sb = sb("dft_sb", [OG * NF, OG * PATCH])
        G = sb("G", [128, 4, 2, 64])
        parts = sb("parts", [128, SEQ])
        fold = sb("fold", [128, D])
        wqk_sb = sb("wqk_sb", [D + 1, 128])
        W2A, W2B = (parts[:, SEQ // 2 * k:SEQ // 2 * (k + 1)].bitcast(F16).rearrange("p (n d) -> p n d", d=D) for k in range(2))
        wv_sb = sb("wv_sb", [D + 1, D])
        h_tok = sb("h_tok", [128, B * TILES + 1, D])
        centred = sb("centred", [128, TILES + 1, D])
        squares = sb("squares", [128, TILES + 1, D])
        normed = sb("normed", [128, TILES, 2, D])
        stats = sb("stats", [128, 5, TILES + 1])
        minus_half = sb("minus_half", [128, TILES + 1])
        xT = sb("xT", [D + 1, SEQ])
        QA = sb("QA", [128, COLS], F16)
        QB = sb("QB", [128, COLS], F16)
        KA = sb("KA", [128, COLS], F16)
        KB = sb("KB", [128, COLS], F16)
        Hh, Hl = ([t[:, 0:4 * SEQ].rearrange("p (r n) -> p r n", r=4) for t in pair] for pair in ((QA, KA), (QB, KB)))
        qtab_sb = sb("qtab_sb", [128, SEQ + B])
        qhi = sb("qhi", [128, SEQ + B], F16)
        qcol = sb("qcol", [128, 2])
        Vh = sb("Vh", [128, B * TILES, D + 1], F16)
        Vl = sb("Vl", [128, B * TILES, D + 1], F16)
        Vc = sb("Vc", [1, D + 1])
        Pc = sb("Pc", [1, SEQ])
        Pz32 = sb("Pz32", [128, B * TILES])
        Pzh = sb("Pzh", [128, B * 33], F16)
        Pzl = sb("Pzl", [128, B * 33], F16)
        Pzc = sb("Pzc", [1, B])
        mpart = sb("mpart", [128, TILES, 3])
        mneg = sb("mneg", [128, TILES], F16)
        mcls = sb("mcls", [1, 4])
        rden = sb("rden", [128, TILES])
        attn = sb("attn", [128, TILES, D])
        FA = sb("FA", [128, CLS + 128], F16)
        w1f = sb("w1f", [128, COLS // 2])
        WA = sb("WA", [128, E * H], F16)
        WB = sb("WB", [128, E * H], F16)
        w2_sb = sb("w2_sb", [128, HT, D])
        b1_sb = sb("b1_sb", [128, HT])
        wT = w1f[:, :].bitcast(F16)
        b2f = sb("b2f", [128, D])
        B2A = sb("B2A", [128, D], F16)
        B2B = sb("B2B", [128, D], F16)
        sel_sb = sb("sel_sb", [128, E // 2, 128], F16)
        wgf = sb("wgf", [128, E])
        GA = sb("GA", [128, E], F16)
        GB = sb("GB", [128, E], F16)
        bg_sb = sb("bg_sb", [128, E])
        before_sb = sb("before_sb", [128, E * E])
        logits = sb("logits", [128, ALL, E])
        rank = sb("rank", [128, ALL, E])
        top = sb("top", [128, ALL])
        expd = sb("expd", [128, ALL, E])
        chosen = sb("chosen", [128, ALL, E])
        csum = sb("csum", [128, 2, ALL])
        weights = sb("weights", [128, ALL, E])
        weights16 = sb("weights16", [128, ALL, E], F16)
        hcls = sb("hcls", [128, HT, B])
        ocls = sb("ocls", [B, E, D])
        scls = sb("scls", [B, D])
        rcls = sb("rcls", [B, 1])

        ps = ctx.enter_context(nc.psum_tensor("ps", [128, 8, 512], F32))

        def banks(first, count=1):
            return ps[:, first:first + count, :].rearrange("p b n -> p (b n)")

        x_landed = [sem(f"x_landed{b}") for b in range(B)]
        x_ahead = sem("x_ahead")
        x_ready = sem("x_ready")
        emb_w_landed = sem("emb_w_landed")
        ident_landed = sem("ident_landed")
        proj_w_landed = sem("proj_w_landed")
        aug_landed = sem("aug_landed")
        ktab_landed = sem("ktab_landed")
        cls_landed = sem("cls_landed")
        ffn_w_landed = sem("ffn_w_landed")
        gate_w_landed = sem("gate_w_landed")
        stored = sem("stored")
        ones_set = sem("ones_set")
        consts_set = sem("consts_set")
        ident16_set = sem("ident16_set")
        emb_w_summed = sem("emb_w_summed")
        emb_w_ready = sem("emb_w_ready")
        qaug_scaled = sem("qaug_scaled")
        qaug_split = sem("qaug_split")
        qaug_ready = sem("qaug_ready")
        w1_hi = sem("w1_hi")
        w1_lo = sem("w1_lo")
        emb_done = sem("emb_done")
        parts_copied = sem("parts_copied")
        tok_done = sem("tok_done")
        tok_copied = sem("tok_copied")
        ln_sum = sem("ln_sum")
        ln_mean = sem("ln_mean")
        ln_centred = sem("ln_centred")
        ln_squared = sem("ln_squared")
        ln_sumsq = sem("ln_sumsq")
        ln_var = sem("ln_var")
        ln_rstd = sem("ln_rstd")
        ln_done = sem("ln_done")
        norm_T = sem("norm_T")
        xT_copied = sem("xT_copied")
        qk_done = sem("qk_done")
        hi_again = sem("hi_again")
        q_hi = sem("q_hi")
        q_lo = sem("q_lo")
        k_hi = sem("k_hi")
        k_lo = sem("k_lo")
        v_done = sem("v_done")
        v_copied = sem("v_copied")
        side_full = [sem("side_full0"), sem("side_full1")]
        side_free = [sem("side_free0"), sem("side_free1")]
        m_ready = sem("m_ready")
        mcls_max = sem("mcls_max")
        first_full = sem("first_full")
        first_free = sem("first_free")
        mcls_ready = sem("mcls_ready")
        score_done = sem("score_done")
        phi_done = sem("phi_done")
        exp_done = sem("exp_done")
        plo_done = sem("plo_done")
        hi_used = sem("hi_used")
        lo_used = sem("lo_used")
        v_hi = sem("v_hi")
        cq_split = sem("cq_split")
        acc_recip = sem("acc_recip")
        acc_free = sem("acc_free")
        attn_added = sem("attn_added")
        cq_scored = sem("cq_scored")
        cq_exp = sem("cq_exp")
        cq_acc = sem("cq_acc")
        cq_recip = sem("cq_recip")
        cq_added = sem("cq_added")
        clstok_cleared = sem("clstok_cleared")
        wcur_cleared = sem("wcur_cleared")
        wT_cleared = sem("wT_cleared")
        b2_cleared = sem("b2_cleared")
        b2_landed = sem("b2_landed")
        b2_hi = sem("b2_hi")
        b2_lo = sem("b2_lo")
        n2_T = sem("n2_T")
        f_hi = sem("f_hi")
        f_lo = sem("f_lo")
        gate_done = sem("gate_done")
        gate_step = sem("gate_step")
        gate_exp = sem("gate_exp")
        w_ready = sem("w_ready")
        wT_done = sem("wT_done")
        wT_copied = sem("wT_copied")
        hid_done = sem("hid_done")
        gelu_done = sem("gelu_done")
        first_done = sem("first_done")
        h_hi = sem("h_hi")
        h_lo = [sem("h_lo_even"), sem("h_lo_odd")]
        w2_hi = sem("w2_hi")
        w2_lo = sem("w2_lo")
        pair_done = sem("pair_done")
        spread_done = sem("spread_done")
        spread_copied = sem("spread_copied")
        term_ready = sem("term_ready")
        sum_ready = sem("sum_ready")
        fold_done = sem("fold_done")
        tokens_done = sem("tokens_done")
        hcls_done = sem("hcls_done")
        hcls_biased = sem("hcls_biased")
        hcls_gelu = sem("hcls_gelu")
        ocls_done = sem("ocls_done")
        ocls_step = sem("ocls_step")

        PART_RING, P_RING, SCORE_RING = 4, 2, 2

        USES = (12, 11)

        def side(b, n, bank):
            return b * USES[bank] + n - 9

        PAIRS = E // 2

        def tile_count(c):
            return TILES if c < B else 1

        def tiles_of(c):
            return slice(c * TILES, c * TILES + tile_count(c))

        def tokens_of(c):
            return slice(c * SEQ, c * SEQ + 128 * tile_count(c))

        def wT_count(c):
            return SEQ if c < B else B

        def wT_cols(c):
            return slice(c * SEQ, c * SEQ + wT_count(c))

        GATE_PARTS = (slice(0, (B - 1) * TILES), slice((B - 1) * TILES, ALL))
        N2 = B + 1

        LAST_SIDE = ("class scores", "T0", "T1", "T2", "G0", "class sums")
        BEFORE = {1: ("W0",), 2: ("S0",), 3: ("W2",), 4: ("S1",), 5: ("G1",), 6: ("S2",), 7: ("W4", "S3")}
        AFTER = {2: ("W1",), 3: ("T3",), 4: ("T4",), 5: ("hidden",), 6: ("W3",), 7: ("outputs",)}

        def high(x):
            return Hh[x % 2][:, x // 2 % 4, :]

        def low(x):
            return Hl[x % 2][:, x // 2 % 4, :]

        def tile_at(x):
            return 2 * (2 * (x // 4) + x % 2) + x % 4 // 2

        def diagonal(t):
            return t[:, :].rearrange("p (b r) -> p b r", b=B)[:, :, 0:4 * TILES:4]

        def g_part(k):
            o = OG * OBANK * k
            m = min(OG * OBANK, 64 - o)
            return o, m, lambda h: ps[64 * h:64 * h + 64, k, 0:PATCH * m].rearrange("p (o h a q) -> p h q a o", h=2, a=2, q=4)[:, h]

        G_PARTS = [g_part(k) for k in range(-(-OGROUPS // OBANK))]

        def apart(engine):
            engine.wait_ge(consts_set, 3)

        block = ctx.enter_context(nc.Block())

        @block.sync
        def _(sp):
            sp.dma_start(wf_sb[:, :, :], wf.rearrange("p (r n) -> p r n", n=128)).then_inc(emb_w_landed, 16)
            ahead = 512 // V
            for h in range(2):
                to = xs[64 * h:64 * h + 64, 0:ahead * 4 * V].rearrange("p (j n) -> p j n", n=4 * V)
                src = x[0].rearrange("c (j h q) v -> h c j (q v)", h=2, q=4)[h]
                sp.dma_start(to, src[:, 0:ahead, :]).then_inc(x_ahead, 16)
            for b in range(B):
                for h in range(2):
                    to = xs[64 * h:64 * h + 64, b * XB:(b + 1) * XB].rearrange("p (j n) -> p j n", n=4 * V)
                    src = x[b].rearrange("c (j h q) v -> h c j (q v)", h=2, q=4)[h]
                    first = 0 if b else ahead
                    sp.dma_start(to[:, first:NP, :], src[:, first:NP, :]).then_inc(x_landed[b], 16)
                    pad = to[:, NP, :].rearrange("p (q v) -> p q v", q=4)
                    sp.dma_start(pad, x[b, :, T - 1:T, :].broadcast_to([C, 4, V])).then_inc(x_landed[b], 16)
                if b >= 1:
                    sp.wait_ge(x_landed[b - 1], 64)
                    sp.sem_inc(x_ready, 1)
            sp.wait_ge(x_landed[B - 1], 64)
            sp.sem_inc(x_ready, 1)
            for b in range(B):
                sp.dma_start(KA[64:128, b * SEQ:(b + 1) * SEQ], ktab[:, 0:SEQ]).then_inc(ktab_landed, 16)
            sp.dma_start(KA[64:128, CLS:COLS], ktab[:, SEQ:SEQ + B]).then_inc(ktab_landed, 16)
            w1_d = w1.rearrange("e d h -> d e h")
            for g in range(2):
                sp.dma_start(w1f[64 * g:64 * g + 64, 0:E * H].rearrange("p (e h) -> p e h", e=E), w1_d).then_inc(ffn_w_landed, 16)
            sp.dma_start(w2_sb[:, :, :], w2.rearrange("e (j p) d -> p (e j) d", p=128)).then_inc(ffn_w_landed, 16)
            sp.dma_start(b1_sb[:, :], b1).then_inc(ffn_w_landed, 16)
            sp.wait_ge(b2_cleared, 1)
            for g in range(2):
                sp.dma_start(b2f[32 * g:32 * g + E, :], b2).then_inc(b2_landed, 16)
            sp.dma_start(sel_sb[:, :, :], sel.rearrange("p (a m) -> p a m", m=128)).then_inc(ffn_w_landed, 16)
            for g in range(2):
                sp.dma_start(wgf[64 * g:64 * g + 64, :], wg).then_inc(gate_w_landed, 16)
            sp.dma_start(bg_sb[:, :], bg.rearrange("(a e) -> a e", a=1).broadcast_to([128, E])).then_inc(gate_w_landed, 16)
            sp.dma_start(before_sb[:, :], before.broadcast_to([128, E * E])).then_inc(gate_w_landed, 16)
            with sp.Fori(0, B - 1) as b:
                sp.wait_ge(tokens_done, b + 1)
                sp.dma_start(out[bass.ds(b, 1), 1:SEQ + 1, :].rearrange("a (i p) d -> p (a i) d", p=128),
                             h_tok[:, bass.ds(b * TILES, TILES), :]).then_inc(stored, 16)
            for k in range(2):
                sp.wait_ge(tokens_done, B + k)
                sp.dma_start(out[B - 1, 1 + 512 * k:513 + 512 * k, :].rearrange("(i p) d -> p i d", p=128),
                             h_tok[:, (B - 1) * TILES + 4 * k:(B - 1) * TILES + 4 * k + 4, :]).then_inc(stored, 16)
            sp.wait_ge(stored, 16 * (B + 2))

        @block.scalar
        def _(act):
            act.dma_start(dft_sb[:, :], dft).then_inc(emb_w_landed, 16)
            act.dma_start(ident32[:, :], ident).then_inc(ident_landed, 16)
            act.wait_ge(clstok_cleared, 1)
            act.dma_start(h_tok[0:B, B * TILES, :], cls_tok[0].broadcast_to([B, D])).then_inc(cls_landed, 16)
            act.dma_start(wqk_sb[:, :], wqk).then_inc(proj_w_landed, 16)
            act.dma_start(wv_sb[:, :], wv).then_inc(proj_w_landed, 16)
            act.dma_start(qtab_sb[96:128, :], qtab).then_inc(aug_landed, 16)
            act.dma_start(qcol[96:128, 0:1], beta).then_inc(aug_landed, 16)
            act.dma_start(qcol[96:128, 1:2], negmask).then_inc(aug_landed, 16)

            act.wait_ge(emb_w_summed, 1)
            for o, m, summed in G_PARTS:
                nc.scalar.activation(G[64:128, :, :, o:o + m], summed(1), ACT.Copy).then_inc(emb_w_ready, 1)

            def square(k, rows, tiles):
                act.wait_ge(ln_centred, k + 1)
                nc.scalar.activation(squares[0:rows, 0:tiles, :], centred[0:rows, 0:tiles, :], ACT.Square).then_inc(ln_squared, 1)

            def copy_parts(b, first):
                act.wait_ge(emb_done, b + 1)
                if not first:
                    act.wait_ge(tok_done, b)
                for a in range(2):
                    rows = slice(64 * a, 64 * a + 64)
                    by_patch = banks(0, 3)[rows, V * a:V * (a + NP)].rearrange("p (n v) -> p v n", v=V)
                    nc.scalar.activation(parts[rows, :].rearrange("p (v n) -> p v n", n=NP), by_patch, ACT.Copy).then_inc(parts_copied, 1)

            def project_hi(k, cols, n):
                act.wait_ge(qk_done, k + 1)
                nc.scalar.activation(QB[0:64, cols], banks(6, 2)[0:64, 0:n], ACT.Copy, scale=QSCALE).then_inc(q_hi, 1)
                nc.scalar.activation(KB[64:128, cols], banks(6, 2)[64:128, 0:n], ACT.Copy).then_inc(k_hi, 1)

            square(0, B, 1)
            copy_parts(0, True)
            project_hi(0, slice(CLS, COLS), B)
            square(1, 128, TILES)
            with act.Fori(0, B - 1) as b:
                copy_parts(b + 1, False)
                project_hi(b + 1, bass.ds(b * SEQ, SEQ), SEQ)
                square(b + 2, 128, TILES)
            project_hi(B, slice((B - 1) * SEQ, B * SEQ), SEQ)
            act.wait_ge(ffn_w_landed, 80)
            nc.scalar.activation(WA[:, :], w1f[:, 0:E * H], ACT.Copy, scale=WSCALE).then_inc(w1_hi, 1)
            act.wait_ge(tok_done, B)
            nc.scalar.activation(W2A, w2_sb[:, :, :], ACT.Copy, scale=WSCALE).then_inc(w2_hi, 1)
            act.wait_ge(gate_w_landed, 64)
            nc.scalar.activation(GA[:, :], wgf[:, :], ACT.Copy, scale=WSCALE).then_inc(w1_hi, 1)
            act.wait_ge(b2_landed, 32)
            nc.scalar.activation(B2A[:, :], b2f[:, :], ACT.Copy).then_inc(b2_hi, 1)

            def row_of_maxima(b):
                for k in range(2):
                    act.wait_ge(side_full[k], side(b, 10, k))
                    nc.scalar.activation(QA[64:65, bass.ds(b * SEQ + 512 * k, 512)], ps[64:65, 6 + k, :],
                                         ACT.Copy).then_inc(side_free[k], 1)

            def exponentials(b, last=False):
                for t in range(TILES):
                    act.wait_ge(score_done, b * TILES + t + 1)
                    act.wait_ge(hi_used, b * TILES + t + 1)
                    nc.scalar.activation(Phi[:, t % PART_RING, :], banks(2 * (t % 2), 2), ACT.Exp).then_inc(phi_done, 1)
                    act.wait_ge(plo_done, b * TILES + t + 1)
                    nc.scalar.activation(P32[:, t % P_RING, :], banks(2 * (t % 2), 2), ACT.Exp).then_inc(exp_done, 1)
                    if t == 0:
                        act.wait_ge(lo_used, b * TILES + PART_RING)
                        for k in range(2):
                            act.wait_ge(side_full[k], side(b, 11, k))
                            nc.scalar.activation(Pc[:, 512 * k:512 * k + 512], ps[0:1, 6 + k, :], ACT.Exp).then_inc(side_free[k], 1)
                    if t == 2 and not (isinstance(b, int) and b == 0):
                        square(N2 + b - 1, 128, TILES)
                    if last and 1 <= t <= len(LAST_SIDE):
                        beside(LAST_SIDE[t - 1])

            def beside(what):
                if what == "class scores":
                    act.wait_ge(consts_set, 3)
                    act.wait_ge(cq_scored, 1)
                    nc.scalar.activation(Pz32[:, :], ps[:, 6, 0:B * TILES], ACT.Exp).then_inc(cq_exp, 1)
                    nc.scalar.activation(diagonal(Pzh), ps[:, 6, 0:B * TILES].rearrange("p (b t) -> p b t", b=B), ACT.Exp).then_inc(cq_exp, 1)
                    nc.scalar.activation(Pzc[:, :], ps[0:1, 6, B * TILES:B * TILES + B], ACT.Exp).then_inc(cq_exp, 1)
                elif what[0] == "T":
                    c = int(what[1])
                    act.wait_ge(n2_T, c + 1)
                    nc.scalar.activation(FA[0:64, tokens_of(c)], banks(6, 2)[0:64, 0:128 * tile_count(c)], ACT.Copy).then_inc(f_hi, 1)
                elif what == "G1":
                    gate_exponentials(1)
                elif what[0] == "W":
                    c = int(what[1])
                    act.wait_ge(wT_cleared, 1)
                    act.wait_ge(wT_done, c + 1)
                    nc.scalar.activation(wT[0:64, wT_cols(c)], banks(6, 2)[0:64, 0:wT_count(c)], ACT.Copy).then_inc(wT_copied, 1)
                elif what[0] == "S":
                    copy_spread(0, int(what[1]))
                elif what == "hidden":
                    act.wait_ge(hcls_biased, 1)
                    nc.scalar.activation(hcls[:, :, :], hcls[:, :, :], ACT.Gelu).then_inc(hcls_gelu, 1)

            def copy_spread(b, p):
                act.wait_ge(spread_done, b * PAIRS + p + 1)
                if not (isinstance(b, int) and b == 0 and p < 2):
                    act.wait_ge(term_ready, 2 * (b * PAIRS + p - 1))
                nc.scalar.activation(wspread[:, p % 2, :], banks(6, 2), ACT.Copy, scale=1.0 / WSCALE).then_inc(spread_copied, 1)

            def gate_exponentials(q):
                s = GATE_PARTS[q]
                act.wait_ge(gate_step, GATE_STEPS * q + 3)
                nc.scalar.activation(expd[:, s, :], chosen[:, s, :], ACT.Exp).then_inc(gate_exp, 1)

            act.sem_inc(exp_done, SCORE_RING)
            row_of_maxima(0)
            exponentials(0)
            row_of_maxima(1)
            with act.Fori(1, B - 1) as b:
                exponentials(b)
                row_of_maxima(b + 1)
            exponentials(B - 1, last=True)
            gate_exponentials(0)

            def gelu(b, x):
                n = tile_at(x % HT)
                act.wait_ge(hid_done, b * HT + x + 1)
                if not (isinstance(b, int) and b == 0 and x < 4):
                    act.wait_ge(h_lo[x % 2], b * (HT // 2) + x // 2 - 1)
                nc.scalar.activation(hid[:, x % 4, :], banks(2 * (x % 2), 2), ACT.Gelu,
                                     bias=b1_sb[:, n:n + 1], scale=1.0 / WSCALE).then_inc(gelu_done, 1)

            def experts(b, first=False, last=False):
                for u in range(HT // 2):
                    for x in (2 * u + 2, 2 * u + 3):
                        if x < HT or not last:
                            gelu(b, x)
                    if first:
                        for what in BEFORE.get(u, ()) + AFTER.get(u, ()):
                            beside(what)
                    elif u % 2 == 1:
                        copy_spread(b, u // 2)

            gelu(0, 0)
            gelu(0, 1)
            square(N2 + B - 1, 128, TILES + 1)
            experts(0, first=True)
            with act.Fori(1, B - 1) as b:
                experts(b)
            experts(B - 1, last=True)
            act.wait_ge(ocls_step, 4)
            act.dma_start(out[:, 0, :], h_tok[0:B, B * TILES, :]).then_inc(stored, 16)

        @block.vector
        def _(dve):
            nc.vector.memset(h_tok[:, B * TILES, :], 0.0).then_inc(clstok_cleared, 1)
            nc.vector.memset(b2f[:, :], 0.0).then_inc(b2_cleared, 1)
            nc.vector.memset(xT[D:D + 1, :], 1.0).then_inc(ones_set, 1)
            nc.vector.memset(QA[64:96, :], 0.0).then_inc(ones_set, 1)
            nc.vector.memset(Vh[:, :, D:D + 1], 1.0).then_inc(ones_set, 1)
            nc.vector.memset(Vl[:, :, D:D + 1], 0.0).then_inc(ones_set, 1)
            nc.vector.memset(Vc[:, D:D + 1], 1.0).then_inc(ones_set, 1)
            dve.wait_ge(ident_landed, 16)
            nc.vector.tensor_copy(ident16[:, :], ident32[:, :]).then_inc(ident16_set, 1)
            nc.vector.tensor_tensor(fold[:, :], ident32[:, 0:D], ident32[:, D:2 * D], ALU.add).then_inc(ident16_set, 1)
            dve.wait_ge(emb_w_summed, 1)
            for o, m, summed in G_PARTS:
                nc.vector.tensor_copy(G[0:64, :, :, o:o + m], summed(0)).then_inc(emb_w_ready, 1)
            dve.wait_ge(aug_landed, 48)
            nc.vector.tensor_scalar(qtab_sb[96:128, :], qtab_sb[96:128, :], qcol[96:128, 0:1], None, ALU.mult).then_inc(qaug_scaled, 1)
            dve.wait_ge(qaug_scaled, 1)
            nc.vector.tensor_copy(qhi[96:128, :], qtab_sb[96:128, :]).then_inc(qaug_split, 1)
            dve.wait_ge(qaug_split, 1)
            nc.vector.scalar_tensor_tensor(QA[96:128, 0:SEQ], qhi[96:128, 0:SEQ], qcol[96:128, 1:2],
                                           qtab_sb[96:128, 0:SEQ], ALU.mult, ALU.add).then_inc(qaug_ready, 1)
            nc.vector.scalar_tensor_tensor(QA[96:128, CLS:COLS], qhi[96:128, SEQ:SEQ + B], qcol[96:128, 1:2],
                                           qtab_sb[96:128, SEQ:SEQ + B], ALU.mult, ALU.add).then_inc(qaug_ready, 1)
            dve.wait_ge(qaug_ready, 1)
            for b in range(1, B):
                nc.vector.tensor_copy(QA[96:128, b * SEQ:(b + 1) * SEQ], QA[96:128, 0:SEQ]).then_inc(qaug_ready, 1)

            def spread(a, shape):
                return a.unsqueeze(2).broadcast_to(shape)

            def norm_centre(k, src, rows, tiles):
                r, s = slice(0, rows), slice(0, tiles)
                nc.vector.tensor_reduce(stats[r, 0, s], src, AX_X, ALU.add).then_inc(ln_sum, 1)
                dve.wait_ge(ln_sum, k + 1)
                nc.vector.tensor_scalar(stats[r, 1, s], stats[r, 0, s], 1.0 / D, None, ALU.mult).then_inc(ln_mean, 1)
                dve.wait_ge(ln_mean, k + 1)
                nc.vector.tensor_tensor(centred[r, s, :], src, spread(stats[r, 1, s], [rows, tiles, D]), ALU.subtract).then_inc(ln_centred, 1)

            def norm_variance(k, rows, tiles):
                r, s = slice(0, rows), slice(0, tiles)
                dve.wait_ge(ln_squared, k + 1)
                nc.vector.tensor_reduce(stats[r, 2, s], squares[r, s, :], AX_X, ALU.add).then_inc(ln_sumsq, 1)
                dve.wait_ge(ln_sumsq, k + 1)
                nc.vector.tensor_scalar(stats[r, 3, s], stats[r, 2, s], 1.0 / D, EPS, ALU.mult, ALU.add).then_inc(ln_var, 1)

            def norm_scale(k, rows, tiles, to=None):
                r, s = slice(0, rows), slice(0, tiles)
                dve.wait_ge(ln_rstd, k + 1)
                nc.vector.tensor_tensor(normed[r, s, 0, :] if to is None else to, centred[r, s, :], spread(stats[r, 4, s], [rows, tiles, D]), ALU.mult).then_inc(ln_done, 1)

            def take_transposed(k, n):
                dve.wait_ge(norm_T, k + 1)
                nc.vector.tensor_copy(xT[0:D, 0:n], banks(4, 2)[0:D, 0:n]).then_inc(xT_copied, 1)

            def project_low_queries(k, cols, n):
                dve.wait_ge(q_hi, k + 1)
                nc.vector.tensor_copy(QA[0:64, cols], QB[0:64, cols]).then_inc(hi_again, 1)
                nc.vector.scalar_tensor_tensor(QB[64:128, cols], banks(6, 2)[0:64, 0:n], QSCALE, QB[0:64, cols],
                                               ALU.mult, ALU.subtract).then_inc(q_lo, 1)

            def project_low_keys(k, cols, n):
                dve.wait_ge(k_hi, k + 1)
                nc.vector.tensor_copy(KA[0:64, cols], KB[64:128, cols]).then_inc(hi_again, 1)
                nc.vector.tensor_tensor(KB[0:64, cols], banks(6, 2)[64:128, 0:n], KB[64:128, cols], ALU.subtract).then_inc(k_lo, 1)

            def project_lo(k, cols, n):
                project_low_queries(k, cols, n)
                project_low_keys(k, cols, n)

            def take_values(k, tiles):
                dve.wait_ge(v_done, k + 1)
                values = ps[:, 4, :].rearrange("p (t d) -> p t d", d=D)
                nc.vector.tensor_copy(Vh[:, tiles, 0:D], values).then_inc(v_hi, 1)
                dve.wait_ge(v_hi, k + 1)
                nc.vector.tensor_tensor(Vl[:, tiles, 0:D], values, Vh[:, tiles, 0:D], ALU.subtract).then_inc(v_copied, 1)

            def take_tokens(b):
                dve.wait_ge(tok_done, b + 1)
                tokens = h_tok[:, bass.ds(b * TILES, TILES), :]
                nc.vector.tensor_copy(tokens, ps[:, 3, :].rearrange("p (t d) -> p t d", d=D)).then_inc(tok_copied, 1)
                apart(dve)
                dve.wait_ge(tok_copied, b + 1)
                norm_centre(b + 1, tokens, 128, TILES)

            for free in (v_copied, q_lo, k_lo):
                dve.sem_inc(free, 1)
            dve.wait_ge(cls_landed, 16)
            norm_centre(0, h_tok[0:B, B * TILES:ALL, :], B, 1)
            norm_variance(0, B, 1)
            norm_scale(0, B, 1)
            take_transposed(0, B)
            project_lo(0, slice(CLS, COLS), B)
            dve.wait_ge(v_done, 1)
            nc.vector.tensor_copy(Vc[:, 0:D], ps[0:1, 4, 0:D]).then_inc(v_copied, 1)
            dve.sem_inc(v_hi, 1)
            take_tokens(0)
            norm_variance(1, 128, TILES)
            norm_scale(1, 128, TILES)
            with dve.Fori(0, B - 1) as b:
                take_transposed(b + 1, SEQ)
                take_tokens(b + 1)
                norm_variance(b + 2, 128, TILES)
                project_low_queries(b + 1, bass.ds(b * SEQ, SEQ), SEQ)
                norm_scale(b + 2, 128, TILES)
                take_values(b + 1, bass.ds(b * TILES, TILES))
                project_low_keys(b + 1, bass.ds(b * SEQ, SEQ), SEQ)

            def first_class_maxima():
                dve.wait_ge(first_full, 1)
                nc.vector.tensor_copy(mpart[:, :, 2], ps[:, 0, 0:TILES]).then_inc(mcls_max, 1)
                nc.vector.tensor_copy(mcls[:, 2:3], ps[0:1, 0, TILES:TILES + 1]).then_inc(first_free, 1)
                dve.wait_ge(first_full, 2)
                nc.vector.tensor_reduce(mcls[:, 0:2], ps[0:1, 2:4, :], AX_X, ALU.max).then_inc(first_free, 1)

            def first_maxima(first, last):
                for i in range(first, last):
                    dve.wait_ge(first_full, 3 + i)
                    nc.vector.tensor_reduce(mpart[:, i, 0:2], ps[:, 2 * (i % 2):2 * (i % 2) + 2, :], AX_X, ALU.max).then_inc(first_free, 1)

            take_transposed(B, SEQ)
            first_class_maxima()
            first_maxima(0, 2)
            project_lo(B, slice((B - 1) * SEQ, B * SEQ), SEQ)
            first_maxima(2, 4)
            take_values(B, slice((B - 1) * TILES, B * TILES))
            first_maxima(4, TILES)

            def class_maxima(b):
                dve.wait_ge(mcls_ready, b)
                dve.wait_ge(side_full[0], side(b, 0, 0))
                nc.vector.tensor_copy(mpart[:, :, 2], ps[:, 6, 0:TILES]).then_inc(mcls_max, 1)
                nc.vector.tensor_copy(mcls[:, 2:3], ps[0:1, 6, TILES:TILES + 1]).then_inc(side_free[0], 1)
                for k in range(2):
                    dve.wait_ge(side_full[k], side(b, 1, k))
                    nc.vector.tensor_reduce(mcls[:, k:k + 1], ps[0:1, 6 + k, :], AX_X, ALU.max).then_inc(side_free[k], 1)

            def tile_maxima(b, first, last):
                for i in range(first, last):
                    for k in range(2):
                        dve.wait_ge(side_full[k], side(b, 2 + i, k))
                        nc.vector.tensor_reduce(mpart[:, i, k:k + 1], ps[:, 6 + k, :], AX_X, ALU.max).then_inc(side_free[k], 1)

            def all_maxima(b):
                if isinstance(b, int) and b == 0:
                    dve.wait_ge(first_free, TILES + 2)
                else:
                    for k in range(2):
                        dve.wait_ge(side_free[k], side(b, 9, k))
                nc.vector.tensor_reduce(mneg[:, :], mpart[:, :, :], AX_X, ALU.max, negate=True).then_inc(m_ready, 1)
                nc.vector.tensor_reduce(QA[64:65, bass.ds(CLS + b, 1)], mcls[:, 0:3], AX_X, ALU.max, negate=True).then_inc(mcls_ready, 1)

            def second_centre(c):
                apart(dve)
                dve.wait_ge(attn_added, c + 2)
                norm_centre(N2 + c, h_tok[:, bass.ds(c * TILES, TILES), :], 128, TILES)

            def second_scale(c):
                norm_scale(N2 + c, 128, TILES, normed2[:, bass.ds(c * TILES, TILES), :])

            def normalise(b):
                sums = ps[:, 4:6, 0:4 * (D + 1)].rearrange("p a (i d) -> p a i d", d=D + 1)
                dve.wait_ge(lo_used, (b + 1) * TILES + PART_RING)
                nc.vector.reciprocal(rden[:, :].rearrange("p (a i) -> p a i", a=2), sums[:, :, :, D]).then_inc(acc_recip, 1)
                dve.wait_ge(acc_recip, b + 1)
                dve.wait_ge(attn_added, b + 1)
                r = rden[:, :].rearrange("p (a i) -> p a i", a=2).unsqueeze(3).broadcast_to([128, 2, 4, D])
                nc.vector.tensor_tensor(attn[:, :, :].rearrange("p (a i) d -> p a i d", a=2), sums[:, :, :, 0:D], r, ALU.mult).then_inc(acc_free, 1)

            def norm_low(c):
                dve.wait_ge(f_hi, c + 1)
                nc.vector.tensor_tensor(FA[64:128, tokens_of(c)], banks(6, 2)[0:64, 0:128 * tile_count(c)],
                                        FA[0:64, tokens_of(c)], ALU.subtract).then_inc(f_lo, 1)

            def step(q, i, ins):
                ins.then_inc(gate_step, 1)
                dve.wait_ge(gate_step, GATE_STEPS * q + i)

            def gate_ranks(q):
                s = GATE_PARTS[q]
                n = s.stop - s.start
                lg = logits[:, s, :]
                flat = lambda t: t[:, s, :, :].rearrange("p t e f -> p t (e f)")
                dve.wait_ge(gate_done, q + 1)
                step(q, 1, nc.vector.scalar_tensor_tensor(lg, ps[:, 6, E * s.start:E * s.stop].rearrange("p (t e) -> p t e", e=E), 1.0 / WSCALE,
                                                          bg_sb[:, :].unsqueeze(1).broadcast_to([128, n, E]), ALU.mult, ALU.add))
                step(q, 2, nc.vector.tensor_reduce(top[:, s], lg, AX_X, ALU.max))
                step(q, 3, nc.vector.tensor_tensor(chosen[:, s, :], lg, top[:, s].unsqueeze(2).broadcast_to([128, n, E]), ALU.subtract))
                step(q, 4, nc.vector.tensor_tensor(diff[:, s, :, :], lg.unsqueeze(2).broadcast_to([128, n, E, E]),
                                                   lg.unsqueeze(3).broadcast_to([128, n, E, E]), ALU.subtract))
                step(q, 5, nc.vector.scalar_tensor_tensor(flat(equal), flat(diff), 0.0, before_sb[:, :].unsqueeze(1).broadcast_to([128, n, E * E]),
                                                          ALU.is_equal, ALU.mult))
                step(q, 6, nc.vector.scalar_tensor_tensor(flat(diff), flat(diff), 0.0, flat(equal), ALU.is_gt, ALU.add))

            def gate_weights(q):
                s = GATE_PARTS[q]
                n = s.stop - s.start
                step(q, 7, nc.vector.tensor_reduce(rank[:, s, :], diff[:, s, :, :], AX_X, ALU.add))
                dve.wait_ge(gate_exp, q + 1)
                step(q, 8, nc.vector.scalar_tensor_tensor(chosen[:, s, :], rank[:, s, :], 2.0, expd[:, s, :], ALU.is_lt, ALU.mult))
                step(q, 9, nc.vector.tensor_reduce(csum[:, 0, s], chosen[:, s, :], AX_X, ALU.add))
                step(q, 10, nc.vector.reciprocal(csum[:, 1, s], csum[:, 0, s]))
                step(q, 11, nc.vector.tensor_tensor(weights[:, s, :], chosen[:, s, :], csum[:, 1, s].unsqueeze(2).broadcast_to([128, n, E]), ALU.mult))
                step(q, 12, nc.vector.tensor_copy(weights16[:, s, :], weights[:, s, :]))
                nc.vector.tensor_copy(wcur[:, s, 0, 0:E], weights16[:, s, :]).then_inc(w_ready, 1)
                nc.vector.tensor_tensor(wcur[:, s, 1, 0:E], weights[:, s, :], weights16[:, s, :], ALU.subtract).then_inc(w_ready, 1)

            def split(b, x):
                dve.wait_ge(gelu_done, b * HT + x + 1)
                if not (isinstance(b, int) and b == 0 and x < 8):
                    before = x // 2 - 4
                    if before % 2 == 0:
                        dve.wait_ge(first_done, b * PAIRS + before // 2 + 1)
                    else:
                        dve.wait_ge(pair_done, b * PAIRS + before // 2 + 1)
                nc.vector.tensor_copy(high(x), hid[:, x % 4, :]).then_inc(h_hi, 1)
                if x % 2 == 1:
                    dve.wait_ge(h_hi, b * HT + x + 1)
                    nc.vector.tensor_tensor(low(x), hid[:, x % 4, :], high(x), ALU.subtract).then_inc(h_lo[1], 1)

            dve.sem_inc(acc_free, 1)
            all_maxima(0)
            dve.wait_ge(w1_hi, 2)
            nc.vector.scalar_tensor_tensor(WB[:, :], w1f[:, 0:E * H], WSCALE, WA[:, :], ALU.mult, ALU.subtract).then_inc(w1_lo, 1)
            nc.vector.scalar_tensor_tensor(GB[:, :], wgf[:, :], WSCALE, GA[:, :], ALU.mult, ALU.subtract).then_inc(w1_lo, 1)
            dve.wait_ge(b2_hi, 1)
            nc.vector.tensor_tensor(B2B[:, :], b2f[:, :], B2A[:, :], ALU.subtract).then_inc(b2_lo, 1)
            dve.wait_ge(w2_hi, 1)
            nc.vector.scalar_tensor_tensor(W2B, w2_sb[:, :, :], WSCALE, W2A, ALU.mult, ALU.subtract).then_inc(w2_lo, 1)
            dve.wait_ge(emb_done, B)
            nc.vector.memset(wcur, 0.0).then_inc(wcur_cleared, 1)
            dve.wait_ge(w1_lo, 1)
            nc.vector.memset(wT[64:128, :], 0.0).then_inc(wT_cleared, 1)

            class_maxima(1)
            tile_maxima(1, 0, TILES)
            all_maxima(1)
            normalise(0)
            with dve.Fori(1, B - 1) as b:
                class_maxima(b + 1)
                tile_maxima(b + 1, 0, 1)
                second_centre(b - 1)
                tile_maxima(b + 1, 1, 2)
                norm_variance(N2 + b - 1, 128, TILES)
                tile_maxima(b + 1, 2, 5)
                second_scale(b - 1)
                tile_maxima(b + 1, 5, TILES)
                all_maxima(b + 1)
                normalise(b)
            c = B - 2
            second_centre(c)
            norm_variance(N2 + c, 128, TILES)
            dve.wait_ge(cq_exp, 3)
            nc.vector.tensor_tensor(diagonal(Pzl), Pz32[:, :].rearrange("p (b t) -> p b t", b=B), diagonal(Pzh), ALU.subtract).then_inc(cq_split, 1)
            norm_low(0)
            second_scale(c)
            for c in range(1, B - 1):
                norm_low(c)
            dve.wait_ge(wcur_cleared, 1)
            gate_ranks(0)
            mine = h_tok[0:B, B * TILES, :]
            dve.wait_ge(cq_acc, 1)
            nc.vector.reciprocal(rcls[:, :], ps[0:B, 7, D:D + 1]).then_inc(cq_recip, 1)
            dve.wait_ge(cq_recip, 1)
            nc.vector.scalar_tensor_tensor(mine, ps[0:B, 7, 0:D], rcls[:, :], mine, ALU.mult, ALU.add).then_inc(cq_added, 1)
            normalise(B - 1)
            dve.wait_ge(attn_added, B + 1)
            dve.wait_ge(cq_added, 1)
            norm_centre(N2 + B - 1, h_tok[:, (B - 1) * TILES:ALL, :], 128, TILES + 1)
            split(0, 0)
            split(0, 1)
            gate_weights(0)

            def add_tokens(b):
                tokens = h_tok[:, bass.ds(b * TILES, TILES), :]
                apart(dve)
                dve.wait_ge(fold_done, b + 1)
                nc.vector.tensor_tensor(tokens, ps[:, 6, :].rearrange("p (t d) -> p t d", d=D), tokens, ALU.add).then_inc(tokens_done, 1)

            def beside(what):
                if what[0] == "T":
                    norm_low(int(what[1]))
                elif what == "G1":
                    gate_ranks(1)
                elif what == "hidden":
                    gate_weights(1)
                    dve.wait_ge(hcls_done, 1)
                    nc.vector.scalar_tensor_tensor(hcls[:, :, :], ps[:, 6, 0:HT * B].rearrange("p (n c) -> p n c", c=B), 1.0 / WSCALE,
                                                   b1_sb[:, :].unsqueeze(2).broadcast_to([128, HT, B]), ALU.mult, ALU.add).then_inc(hcls_biased, 1)
                elif what == "outputs":
                    dve.wait_ge(ocls_done, 1)
                    nc.vector.tensor_tensor(ocls[:, :, :], ps[0:B, 7, :].rearrange("p (e d) -> p e d", d=D),
                                            weights[0:B, B * TILES, :].unsqueeze(2).broadcast_to([B, E, D]), ALU.mult).then_inc(ocls_step, 1)
                    nc.vector.tensor_tensor(mine, ps[0:B, 6, 0:D], mine, ALU.add).then_inc(ocls_step, 1)
                    dve.wait_ge(ocls_step, 2)
                    nc.vector.tensor_reduce(scls[:, :], ocls[:, :, :].rearrange("p e d -> p d e"), AX_X, ALU.add).then_inc(ocls_step, 1)
                    dve.wait_ge(ocls_step, 3)
                    nc.vector.tensor_tensor(mine, mine, scls[:, :], ALU.add).then_inc(ocls_step, 1)

            def term(b, p):
                dve.wait_ge(spread_copied, b * PAIRS + p + 1)
                dve.wait_ge(pair_done, b * PAIRS + p + 1)
                if p > 0 and not (isinstance(b, int) and b == 0 and p == 1):
                    dve.wait_ge(sum_ready, b * (PAIRS - 1) + p - 1)
                for k in range(2):
                    part = slice(512 * k, 512 * k + 512)
                    nc.vector.tensor_tensor((eterm if p else esum)[:, part], ps[:, 4 + k, :], wspread[:, p % 2, part], ALU.mult).then_inc(term_ready, 1)

            def experts(b, first=False, last=False):
                for u in range(HT // 2):
                    more = u < HT // 2 - 1 or not last
                    if more:
                        split(b, 2 * u + 2)
                    if u == 0 and not first:
                        term(b - 1, PAIRS - 1)
                    elif u > 0 and u % 2 == 0:
                        term(b, u // 2 - 1)
                    if more:
                        split(b, 2 * u + 3)
                    if first and u == 0:
                        norm_variance(N2 + B - 1, 128, TILES + 1)
                        norm_scale(N2 + B - 1, 128, TILES + 1, normed2[:, (B - 1) * TILES:ALL, :])
                    if first:
                        for what in BEFORE.get(u, ()) + AFTER.get(u, ()):
                            beside(what)
                    elif u == 1:
                        add_tokens(b - 1)

            experts(0, first=True)
            with dve.Fori(1, B - 1) as b:
                experts(b)
            experts(B - 1, last=True)
            p = PAIRS - 1
            dve.wait_ge(spread_copied, B * PAIRS)
            dve.wait_ge(pair_done, B * PAIRS)
            dve.wait_ge(sum_ready, B * p - 1)
            for k in range(2):
                part = slice(512 * k, 512 * k + 512)
                nc.vector.tensor_tensor(eterm[:, part], ps[:, 4 + k, :], wspread[:, p % 2, part], ALU.mult).then_inc(term_ready, 1)
                dve.wait_ge(term_ready, 2 * B * PAIRS - 1 + k)
                nc.vector.tensor_tensor(esum[:, part], esum[:, part], eterm[:, part], ALU.add).then_inc(sum_ready, 1)
            for k in range(2):
                tokens = h_tok[:, (B - 1) * TILES + 4 * k:(B - 1) * TILES + 4 * k + 4, :]
                dve.wait_ge(fold_done, B + k)
                nc.vector.tensor_tensor(tokens, ps[:, 6 + k, 256 * k:256 * k + 256].rearrange("p (t d) -> p t d", d=D), tokens,
                                        ALU.add).then_inc(tokens_done, 1)

        @block.gpsimd
        def _(pool):
            nc.gpsimd.memset(minus_half[:, :], -0.5).then_inc(consts_set, 1)
            nc.gpsimd.memset(Pzh[:, :], 0.0).then_inc(consts_set, 1)
            nc.gpsimd.memset(Pzl[:, :], 0.0).then_inc(consts_set, 1)
            nc.gpsimd.memset(normed[:, :, 1, :], 0.0).then_inc(ones_set, 1)

            def rstd(k, rows, tiles):
                pool.wait_ge(ln_var, k + 1)
                r, s = slice(0, rows), slice(0, tiles)
                nc.gpsimd.tensor_tensor(stats[r, 4, s], stats[r, 3, s], minus_half[r, s], ALU.pow).then_inc(ln_rstd, 1)

            pool.wait_ge(consts_set, 3)
            rstd(0, B, 1)
            with pool.Fori(1, B + 1) as k:
                rstd(k, 128, TILES)

            pool.sem_inc(attn_added, 1)

            def add_attention(b):
                apart(pool)
                pool.wait_ge(acc_free, b + 2)
                tokens = h_tok[:, bass.ds(b * TILES, TILES), :]
                nc.gpsimd.tensor_tensor(tokens, tokens, attn[:, :, :], ALU.add).then_inc(attn_added, 1)

            def low_parts(b, first, last):
                for t in range(first, last):
                    pool.wait_ge(exp_done, b * TILES + t + 1 + SCORE_RING)
                    pool.wait_ge(lo_used, b * TILES + t + 1)
                    nc.gpsimd.tensor_tensor(Plo[:, t % PART_RING, :], P32[:, t % P_RING, :], Phi[:, t % PART_RING, :],
                                            ALU.subtract).then_inc(plo_done, 1)

            pool.sem_inc(plo_done, P_RING)
            low_parts(0, 0, TILES)
            add_attention(0)
            with pool.Fori(1, B) as b:
                low_parts(b, 0, 3)
                rstd(N2 + b - 1, 128, TILES)
                low_parts(b, 3, TILES)
                add_attention(b)

            def split_low(b, x):
                pool.wait_ge(h_hi, b * HT + x + 1)
                nc.gpsimd.tensor_tensor(low(x), hid[:, x % 4, :], high(x), ALU.subtract).then_inc(h_lo[0], 1)

            def add_term(b, p):
                pool.wait_ge(term_ready, 2 * (b * PAIRS + p + 1))
                nc.gpsimd.tensor_tensor(esum, esum, eterm, ALU.add).then_inc(sum_ready, 1)

            def experts(b, first=False, last=False):
                for u in range(HT // 2):
                    if 2 * u + 2 < HT or not last:
                        split_low(b, 2 * u + 2)
                    if first and u == 0:
                        rstd(N2 + B - 1, 128, TILES + 1)
                    if u == 0 and not first:
                        add_term(b - 1, PAIRS - 1)
                    elif u >= 4 and u % 2 == 0:
                        add_term(b, u // 2 - 1)

            split_low(0, 0)
            experts(0, first=True)
            with pool.Fori(1, B - 1) as b:
                experts(b)
            experts(B - 1, last=True)

        @block.tensor
        def _(pe):
            pe.wait_ge(emb_w_landed, 32)
            for r in range(OGROUPS):
                at = OG * PATCH * (r % OBANK)
                last = nc.tensor.matmul(ps[:, r // OBANK, at:at + OG * PATCH], wf_sb[:, r, :], dft_sb[:, :], start=True, stop=True)
            last.then_inc(emb_w_summed, 1)

            def embed(b, first, between=None):
                if first:
                    pe.wait_ge(x_ahead, 32)
                else:
                    pe.wait_ge(x_ready, b + 1)
                    pe.wait_ge(parts_copied, 2 * b)
                blocks = xs[:, bass.ds(b * XB, XB)].rearrange("p (j q v) -> p j q v", q=4, v=V)
                for c, j0 in enumerate(range(0, NBLK, 8)):
                    j1 = min(j0 + 8, NBLK)
                    if first and c == 1:
                        pe.wait_ge(x_ready, b + 1)
                    for q in range(4):
                        if between and (c, q) == (2, 0):
                            between()
                        last = nc.tensor.matmul(ps[:, c, 0:V * (j1 - j0)], G[:, q, :, :].rearrange("p a o -> p (a o)"),
                                                blocks[:, j0:j1, q, :], start=(q == 0), stop=(q == 3))
                last.then_inc(emb_done, 1)

            def sum_halves(b, first):
                pe.wait_ge(parts_copied, 2 * (b + 1))
                if not first:
                    pe.wait_ge(tok_copied, b)
                for i in range(TILES):
                    last = nc.tensor.matmul(ps[:, 3, D * i:D * i + D], parts[:, 128 * i:128 * i + 128], fold[:, :], start=True, stop=True)
                last.then_inc(tok_done, 1)

            def transposed(k, tiles, rows):
                pe.wait_ge(ln_done, k + 1)
                pe.wait_ge(v_copied, k + 1)
                for i in range(tiles):
                    last = nc.tensor.transpose(banks(4, 2)[:, 128 * i:128 * i + rows], normed[0:rows, i, :, :].rearrange("p g d -> p (g d)"), ident32[0:rows, 0:rows])
                last.then_inc(norm_T, 1)

            def project_queries_keys(k, tiles, rows):
                n = rows * tiles
                pe.wait_ge(xT_copied, k + 1)
                pe.wait_ge(q_lo, k + 1)
                pe.wait_ge(k_lo, k + 1)
                for c in range(0, n, 512):
                    m = min(512, n - c)
                    last = nc.tensor.matmul(ps[:, 6 + c // 512, 0:m], wqk_sb[:, :], xT[:, c:c + m], start=True, stop=True)
                last.then_inc(qk_done, 1)

            def project_values(k, tiles, rows):
                for i in range(tiles):
                    last = nc.tensor.matmul(ps[0:rows, 4, D * i:D * i + D], xT[:, i * 128:i * 128 + rows], wv_sb[:, :], start=True, stop=True)
                last.then_inc(v_done, 1)

            pe.wait_ge(emb_w_ready, 6)
            embed(0, True)
            pe.wait_ge(ident_landed, 16)
            pe.wait_ge(ident16_set, 2)
            pe.wait_ge(proj_w_landed, 32)
            pe.wait_ge(ones_set, 6)
            transposed(0, 1, B)
            project_queries_keys(0, 1, B)
            project_values(0, 1, B)
            sum_halves(0, True)
            with pe.Fori(0, B - 1) as b:
                embed(b + 1, False, between=lambda: transposed(b + 1, TILES, 128))
                project_queries_keys(b + 1, TILES, 128)
                sum_halves(b + 1, False)
                project_values(b + 1, TILES, 128)

            def first_class_scores():
                pe.wait_ge(parts_copied, 2 * B)
                pe.wait_ge(tok_copied, B)
                for i in range(TILES):
                    nc.tensor.matmul(ps[:, 0, i:i + 1], QA[:, 128 * i:128 * i + 128], KA[:, CLS:CLS + 1], start=True, stop=True)
                nc.tensor.matmul(ps[0:1, 0, TILES:TILES + 1], QA[:, COLS - 1:COLS], KA[:, CLS:CLS + 1],
                                 start=True, stop=True).then_inc(first_full, 1)
                for k in range(2):
                    last = nc.tensor.matmul(ps[0:1, 2 + k, :], QA[:, COLS - 1:COLS], KA[:, 512 * k:512 * k + 512], start=True, stop=True)
                last.then_inc(first_full, 1)

            def first_scores_of_tiles(first, last):
                for i in range(first, last):
                    pe.wait_ge(first_free, i + 1)
                    for k in range(2):
                        ins = nc.tensor.matmul(ps[:, 2 * (i % 2) + k, :], QA[:, 128 * i:128 * i + 128], KA[:, 512 * k:512 * k + 512],
                                               start=True, stop=True)
                    ins.then_inc(first_full, 1)

            pe.wait_ge(hi_again, 4)
            pe.wait_ge(qaug_ready, B + 1)
            pe.wait_ge(ktab_landed, 16 * (B + 1))
            first_class_scores()
            transposed(B, TILES, 128)
            first_scores_of_tiles(0, 1)
            project_queries_keys(B, TILES, 128)
            first_scores_of_tiles(1, 2)
            project_values(B, TILES, 128)
            first_scores_of_tiles(2, TILES)

            def cols(b, t, n):
                return bass.ds(b * SEQ + t, n)

            def own(b, turn, bank):
                before_it = side(b, turn, bank) - 1
                if not (isinstance(before_it, int) and before_it == 0):
                    pe.wait_ge(side_free[bank], before_it)

            def turn(b, n):
                if n == 0:
                    own(b, n, 0)
                    for i in range(TILES):
                        nc.tensor.matmul(ps[:, 6, i:i + 1], QA[:, cols(b, 128 * i, 128)], KA[:, CLS:CLS + 1], start=True, stop=True)
                    nc.tensor.matmul(ps[0:1, 6, TILES:TILES + 1], QA[:, COLS - 1:COLS], KA[:, CLS:CLS + 1],
                                     start=True, stop=True).then_inc(side_full[0], 1)
                elif n == 1:
                    for k in range(2):
                        own(b, n, k)
                        nc.tensor.matmul(ps[0:1, 6 + k, :], QA[:, COLS - 1:COLS], KA[:, cols(b, 512 * k, 512)],
                                         start=True, stop=True).then_inc(side_full[k], 1)
                elif n < 10:
                    for k in range(2):
                        own(b, n, k)
                        nc.tensor.matmul(ps[:, 6 + k, :], QA[:, cols(b, 128 * (n - 2), 128)], KA[:, cols(b, 512 * k, 512)],
                                         start=True, stop=True).then_inc(side_full[k], 1)
                elif n == 10:
                    pe.wait_ge(m_ready, b + 1)
                    for k in range(2):
                        own(b, n, k)
                        for i in range(4):
                            last = nc.tensor.matmul(ps[64:65, 6 + k, 128 * i:128 * i + 128], mneg[:, 4 * k + i:4 * k + i + 1],
                                                    ident16[:, :], start=True, stop=True)
                        last.then_inc(side_full[k], 1)
                else:
                    for k in range(2):
                        own(b, n, k)
                    for k in range(2):
                        for g, (KX, QX) in enumerate(((KA, QA), (KB, QB))):
                            last = nc.tensor.matmul(ps[0:1, 6 + k, :], KX[:, CLS:CLS + 1], QX[:, cols(b, 512 * k, 512)],
                                                    start=(g == 0), stop=(g == 1))
                        last.then_inc(side_full[k], 1)

            def scores(b, t):
                pe.wait_ge(exp_done, b * TILES + t + 1)
                pair = 2 * (t % 2)
                for g, (KX, QX) in enumerate(((KA, QA), (KB, QB))):
                    for k in range(2):
                        last = nc.tensor.matmul(ps[:, pair + k, :], KX[:, cols(b, 128 * t, 128)], QX[:, cols(b, 512 * k, 512)],
                                                start=(g == 0), stop=(g == 1))
                last.then_inc(score_done, 1)

            def sum_tile(i):
                return ps[:, 4 + i // 4, (D + 1) * (i % 4):(D + 1) * (i % 4 + 1)]

            def values_high(b, t):
                pe.wait_ge(phi_done, b * TILES + t + 1)
                if t == 0:
                    pe.wait_ge(acc_free, b + 1)
                for i in range(TILES):
                    for g, VX in enumerate((Vh, Vl)):
                        last = nc.tensor.matmul(sum_tile(i), Phi[:, t % PART_RING, 128 * i:128 * i + 128], VX[:, bass.ds(b * TILES + t, 1), :],
                                                start=(t == 0 and i % 4 == 0 and g == 0), stop=False, skip_group_check=True)
                last.then_inc(hi_used, 1)

            def values_low(b, t):
                pe.wait_ge(plo_done, b * TILES + t + 1 + P_RING)
                for i in range(TILES):
                    last = nc.tensor.matmul(sum_tile(i), Plo[:, t % PART_RING, 128 * i:128 * i + 128], Vh[:, bass.ds(b * TILES + t, 1), :],
                                            start=False, stop=(t == TILES - 1), skip_group_check=True)
                last.then_inc(lo_used, 1)

            def class_values(b):
                for k in range(2):
                    pe.wait_ge(side_free[k], side(b, 11, k))
                for i in range(TILES):
                    nc.tensor.matmul(sum_tile(i), Pc[:, 128 * i:128 * i + 128], Vc[:, :],
                                     start=False, stop=False, skip_group_check=True)

            def first_scores(b):
                for k in range(2):
                    pe.wait_ge(side_free[k], side(b, 10, k))
                scores(b, 0)
                scores(b, 1)

            def attend(b, more):
                turn(b, 11)
                for t in range(TILES):
                    turns = TURNS[t] if more else []
                    for n in turns[0:-1]:
                        turn(b + 1, n)
                    values_high(b, t)
                    for n in turns[-1:]:
                        turn(b + 1, n)
                    if not more and t < len(LAST_SIDE):
                        beside(LAST_SIDE[t])
                    if t + 2 < TILES:
                        scores(b, t + 2)
                    if t > 0:
                        values_low(b, t - 1)
                class_values(b)
                if more:
                    first_scores(b + 1)
                values_low(b, TILES - 1)

            def transposed_norm(c):
                pe.wait_ge(ln_done, N2 + min(c, B - 1) + 1)
                for i in range(tile_count(c)):
                    last = nc.tensor.transpose(banks(6, 2)[0:D, 128 * i:128 * i + 128], normed2[:, c * TILES + i, :], ident32[:, :])
                last.then_inc(n2_T, 1)

            def gate(q):
                pe.wait_ge(w1_lo, 2)
                s = GATE_PARTS[q]
                for i in range(s.start, s.stop):
                    for g, W in enumerate((GA, GB)):
                        last = nc.tensor.matmul(ps[:, 6, E * i:E * i + E], FA[:, 128 * i:128 * i + 128], W[:, :], start=(g == 0), stop=(g == 1))
                last.then_inc(gate_done, 1)

            def transposed_weights(c):
                pe.wait_ge(w_ready, 2 if c < B - 1 else 4)
                for i in range(tile_count(c)):
                    last = nc.tensor.transpose(banks(6, 2)[0:64, 128 * i:128 * i + 128],
                                               wcur[:, c * TILES + i, :, :].rearrange("p g e -> p (g e)"), ident32[:, :])
                last.then_inc(wT_done, 1)

            def class_scores():
                pe.wait_ge(mcls_ready, B)
                for k in range(2):
                    pe.wait_ge(side_free[k], side(B - 1, 11, k))
                for u in range(B * TILES):
                    for g, (KX, QX) in enumerate(((KA, QA), (KB, QB))):
                        nc.tensor.matmul(ps[:, 6, u:u + 1], KX[:, 128 * u:128 * u + 128], QX[:, CLS + u // TILES:CLS + u // TILES + 1],
                                         start=(g == 0), stop=(g == 1))
                for g, (KX, QX) in enumerate(((KA, QA), (KB, QB))):
                    last = nc.tensor.matmul(ps[0:1, 6, B * TILES:B * TILES + B], KX[:, CLS:CLS + 1], QX[:, CLS:COLS], start=(g == 0), stop=(g == 1))
                last.then_inc(cq_scored, 1)

            def class_sums():
                pe.wait_ge(cq_split, 1)
                for u in range(B * TILES):
                    bb, t = divmod(u, TILES)
                    at = 33 * bb + 4 * t - bb
                    for g, (PX, VX) in enumerate(((Pzh, Vh), (Pzh, Vl), (Pzl, Vh))):
                        nc.tensor.matmul(ps[0:B, 7, 0:D + 1], PX[:, at:at + B], VX[:, u, :], start=(u == 0 and g == 0), stop=False)
                nc.tensor.matmul(ps[0:B, 7, 0:D + 1], Pzc[:, :], Vc[:, :], start=False, stop=True).then_inc(cq_acc, 1)

            def class_hidden():
                for n in range(HT):
                    for g, W in enumerate((WA, WB)):
                        last = nc.tensor.matmul(ps[:, 6, B * n:B * n + B], W[:, 128 * n:128 * n + 128], FA[:, CLS:COLS], start=(g == 0), stop=(g == 1))
                last.then_inc(hcls_done, 1)

            def class_outputs():
                pe.wait_ge(hcls_gelu, 1)
                pe.wait_ge(b2_lo, 1)
                for g, W in enumerate((B2A, B2B)):
                    nc.tensor.matmul(ps[0:B, 6, 0:D], wT[:, CLS:COLS], W[:, :], start=(g == 0), stop=(g == 1))
                for e in range(E):
                    for j in range(2):
                        last = nc.tensor.matmul(ps[0:B, 7, D * e:D * e + D], hcls[:, 2 * e + j, :], w2_sb[:, 2 * e + j, :], start=(j == 0), stop=(j == 1))
                last.then_inc(ocls_done, 1)

            def taken(what):
                n = int(what[1]) if what[1].isdigit() else 0
                pe.wait_ge(*{"class scores": (cq_exp, 3), "class sums": (cq_added, 1), "hidden": (hcls_biased, 1), "T": (f_lo, n + 1),
                             "G": (gate_step, GATE_STEPS * n + 1), "W": (wT_copied, n + 1), "S": (spread_copied, n + 1)}[what if len(what) > 2 else what[0]])

            held = [None]

            def beside(what):
                if held[0]:
                    taken(held[0])
                held[0] = what
                {"class scores": class_scores, "class sums": class_sums, "hidden": class_hidden, "outputs": class_outputs,
                 "T": lambda: transposed_norm(int(what[1])), "G": lambda: gate(int(what[1])), "W": lambda: transposed_weights(int(what[1])),
                 "S": lambda: spread_weights(0, int(what[1]))}[what if len(what) > 2 else what[0]]()

            TURNS = [[0, 1], [2, 3], [4], [5, 6], [7], [8], [9], [10]]
            pe.sem_inc(hi_used, PART_RING)
            pe.sem_inc(lo_used, PART_RING)
            pe.wait_ge(q_lo, B + 2)
            pe.wait_ge(k_lo, B + 2)
            pe.wait_ge(hi_again, 2 * (B + 1))
            pe.wait_ge(v_copied, B + 2)
            pe.wait_ge(qaug_ready, B + 1)
            pe.wait_ge(ktab_landed, 16 * (B + 1))
            turn(0, 10)
            first_scores(0)
            with pe.Fori(0, B - 1) as b:
                attend(b, True)
            attend(B - 1, False)

            def hidden(b, x):
                n = tile_at(x % HT)
                if not (isinstance(b, int) and b == 0 and x < 2):
                    pe.wait_ge(gelu_done, b * HT + x - 1)
                for g, W in enumerate((WA, WB)):
                    for k in range(2):
                        last = nc.tensor.matmul(ps[:, 2 * (x % 2) + k, :], W[:, 128 * n:128 * n + 128], FA[:, cols(b + x // HT, 512 * k, 512)],
                                                start=(g == 0), stop=(g == 1))
                last.then_inc(hid_done, 1)

            def outputs(b, u):
                for o in range(2):
                    pe.wait_ge(h_lo[o], b * (HT // 2) + u + 1)
                if isinstance(b, int) and b == u == 0:
                    pe.wait_ge(acc_free, B + 1)
                for k in range(2):
                    if u % 2 == 0 and not (isinstance(b, int) and b == u == 0):
                        pe.wait_ge(term_ready, 2 * (b * PAIRS + u // 2 - 1) + k + 1)
                    for g, (W, part) in enumerate(((W2A, high), (W2B, high), (W2A, low))):
                        for o in range(2):
                            x = 2 * u + o
                            last = nc.tensor.matmul(ps[64 * o:64 * o + 64, 4 + k, :], W[:, tile_at(x), :], part(x)[:, 512 * k:512 * k + 512],
                                                    start=(u % 2 == 0 and g == 0), stop=(u % 2 == 1 and g == 2))
                if u % 2 == 1:
                    last.then_inc(pair_done, 1)
                else:
                    last.then_inc(first_done, 1)

            def spread_weights(b, p):
                for k in range(2):
                    last = nc.tensor.matmul(ps[:, 6 + k, :], sel_sb[:, p, :], wT[:, cols(b, 512 * k, 512)], start=True, stop=True)
                last.then_inc(spread_done, 1)

            def fold_sum(b, tiles=range(TILES), bank=6):
                for i in tiles:
                    to = ps[:, bank, D * i:D * i + D]
                    nc.tensor.matmul(to, esum[:, 128 * i:128 * i + 128], fold[:, :], start=True, stop=False)
                    nc.tensor.matmul(to, wT[:, cols(b, 128 * i, 128)], B2A[:, :], start=False, stop=False)
                    last = nc.tensor.matmul(to, wT[:, cols(b, 128 * i, 128)], B2B[:, :], start=False, stop=True)
                last.then_inc(fold_done, 1)

            def experts(b, first=False, last=False):
                for u in range(HT // 2):
                    for x in (2 * u + 2, 2 * u + 3):
                        if x < HT or not last:
                            hidden(b, x)
                    if first:
                        for what in BEFORE.get(u, ()):
                            beside(what)
                    elif u % 2 == 1:
                        p = u // 2
                        pe.wait_ge(spread_copied, b * PAIRS + p)
                        if p == 0:
                            pe.wait_ge(ocls_step, 2)
                        if p == 1:
                            pe.wait_ge(tokens_done, b)
                        spread_weights(b, p)
                    if u > 0:
                        outputs(b, u - 1)
                    elif not first:
                        outputs(b - 1, HT // 2 - 1)
                    if first:
                        for what in AFTER.get(u, ()):
                            beside(what)
                    elif u == 1:
                        pe.wait_ge(spread_copied, b * PAIRS + 1)
                        pe.wait_ge(sum_ready, b * (PAIRS - 1))
                        fold_sum(b - 1)

            pe.wait_ge(ffn_w_landed, 80)
            pe.wait_ge(w2_lo, 1)
            pe.wait_ge(exp_done, B * TILES + SCORE_RING)
            hidden(0, 0)
            hidden(0, 1)
            experts(0, first=True)
            with pe.Fori(1, B - 1) as b:
                experts(b)
            experts(B - 1, last=True)
            outputs(B - 1, HT // 2 - 1)
            pe.wait_ge(spread_copied, B * PAIRS)
            for k in range(2):
                pe.wait_ge(sum_ready, B * (PAIRS - 1) + k)
                fold_sum(B - 1, range(4 * k, 4 * k + 4), 6 + k)


def _tables():
    f, p = np.arange(PATCH // 2 + 1)[:, None], np.arange(PATCH)[None, :]
    angle = 2 * np.pi * f * p / PATCH
    by_step = np.concatenate([np.cos(angle), -np.sin(angle)]) / np.sqrt(PATCH)
    one = by_step.reshape(NF, 2, 2, 4).transpose(0, 2, 1, 3).reshape(NF, PATCH)
    dft = np.kron(np.eye(OG), one)
    pos = np.concatenate([np.arange(1, SEQ + 1), np.zeros(B)])
    trig = np.stack([g(2 * np.pi * pos / period) for period in PERIODS for g in (np.cos, np.sin)])
    hi = trig.astype(np.float16)
    lo = (trig - hi).astype(np.float16)
    qtab = np.zeros((32, SEQ + B), np.float32)
    qtab[0:12] = np.tile(trig, (3, 1))
    negmask = np.zeros((32, 1), np.float32)
    negmask[8:12] = -1
    ktab = np.zeros((64, SEQ + B), np.float16)
    ktab[0] = 1
    ktab[32:44] = np.concatenate([hi, lo, hi])
    before = (np.arange(E)[None, :] < np.arange(E)[:, None]).astype(np.float32).reshape(1, E * E)
    sel = np.zeros((128, E // 2, 128), np.float16)
    for e in range(E):
        for g in range(2):
            sel[32 * g + e, e // 2, 64 * (e % 2):64 * (e % 2) + 64] = 1
    return {"sel": sel.reshape(128, -1), "dft": dft.astype(np.float32), "ident": np.eye(128, dtype=np.float32), "qtab": qtab, "ktab": ktab,
            "negmask": negmask, "before": before}


def kernel(x, cls_tok, L0_tok_W, L0_attn_Wq, L0_attn_bq, L0_attn_Wk, L0_attn_bk, L0_attn_Wv, L0_attn_bv, L0_attn_beta,
           L0_ffn_Wg, L0_ffn_bg, L0_ffn_W1, L0_ffn_b1, L0_ffn_W2, L0_ffn_b2):
    import concourse.bacc as bacc
    from concourse.bass_utils import run_bass_kernel_spmd

    def with_bias(w, b):
        w, b = np.asarray(w), np.asarray(b)
        return np.concatenate([w.T, b[None, :]])

    w = np.asarray(L0_tok_W).reshape(64, NF, C)
    wf = np.zeros((OGROUPS * OG, NF, 2, C), w.dtype)
    wf[0:64] = w[:, :, None, :]
    beta = np.asarray(L0_attn_beta)
    zeros = np.zeros((20, 1), np.float32)
    arrays = {
        "x": x, "cls_tok": cls_tok,
        "wf": wf.reshape(OGROUPS, OG, NF, 2 * C).transpose(1, 2, 0, 3).reshape(OG * NF, OGROUPS * 2 * C),
        "wqk": np.concatenate([with_bias(L0_attn_Wq, L0_attn_bq), with_bias(L0_attn_Wk, L0_attn_bk)], axis=1),
        "wv": with_bias(L0_attn_Wv, L0_attn_bv),
        "beta": np.concatenate([beta[[0, 0, 1, 1] * 3][:, None], zeros]),
        "wg": L0_ffn_Wg, "bg": L0_ffn_bg, "w1": L0_ffn_W1,
        "b1": np.asarray(L0_ffn_b1).reshape(HT, 128).T,
        "w2": L0_ffn_W2, "b2": L0_ffn_b2,
    }
    arrays.update(_tables())
    arrays = {k: np.ascontiguousarray(v) for k, v in arrays.items()}
    nc = bacc.Bacc("TRN2", target_bir_lowering=False, num_devices=1)
    aps = {k: nc.dram_tensor(f"{k}_dram", v.shape, mybir.dt.from_np(v.dtype), kind="ExternalInput").ap() for k, v in arrays.items()}
    out = nc.dram_tensor("out_dram", (B, SEQ + 1, D), F32, kind="ExternalOutput").ap()
    build(nc, out=out, **aps)
    r = run_bass_kernel_spmd(nc, [{f"{k}_dram": v for k, v in arrays.items()}], core_ids=[0])
    return r.results[0]["out_dram"]
```
